# Optimizing a Trainium2 kernel written in Bass

```python
import numpy as np
import jax
import jax.numpy as jnp

def _softmax(x, axis=-1):
    return jax.nn.softmax(x, axis=axis)

def _gelu(x):
    return jax.nn.gelu(x, approximate=True)

def _silu(x):
    return jax.nn.silu(x)

def _sigmoid(x):
    return jax.nn.sigmoid(x)

def _layernorm(x, axis=-1, eps=1e-05):
    m = jnp.mean(x, axis=axis, keepdims=True)
    v = jnp.var(x, axis=axis, keepdims=True)
    return (x - m) / jnp.sqrt(v + eps)

def _scatter_add(tgt, idx, src, axis=0):
    return tgt.at[idx].add(src)

def _segment_sum(src, seg, n):
    return jax.ops.segment_sum(src, seg, n)
kernel_name = 'mk_vit_tower_postln_d1_tok_img256_r4_26732d'

def setup_inputs(seed: int=0):
    np.random.seed(seed)
    _w = jnp.asarray

    def _rec_inputs():
        import jax
        import jax.numpy as jnp
        _rk = jax.random.key(seed)
        x = -7.10856e-05 + 0.999911 * jax.random.normal(jax.random.fold_in(_rk, 1), (2, 64, 128, 64), jnp.float32)
        return x
    x = _rec_inputs()

    def _L0_tok_setup():
        import jax, jax.numpy as jnp
        import numpy as np
        PATCH_LEN = 16
        STRIDE = 8
        PAD = 8
        key = jax.random.key(seed)
        k1, k2 = jax.random.split(key)
        x = jax.random.normal(k1, (32, 64, 128, 64), dtype=jnp.float32)
        in_feat = 64 * (PATCH_LEN // 2 + 1) * 2
        W = jax.random.normal(k2, (64, in_feat), dtype=jnp.float32) * 0.02
        return {'x': x, 'W': W}
    _L0_tok_all = _L0_tok_setup()
    _L0_tok_in = {k: v for k, v in _L0_tok_all.items() if k in ('W',)}
    del _L0_tok_all

    def _L0_attn_setup():
        import jax, jax.numpy as jnp
        import numpy as np
        key = jax.random.key(seed)
        ks = jax.random.split(key, 4)
        B, S, D = (4, 1024, 64)
        x = jax.random.normal(ks[0], (B, S, D), dtype=jnp.float32)
        Wq = jax.random.normal(ks[1], (D, D), dtype=jnp.float32) * 0.02
        Wk = jax.random.normal(ks[2], (D, D), dtype=jnp.float32) * 0.02
        Wv = jax.random.normal(ks[3], (D, D), dtype=jnp.float32) * 0.02
        bq = jnp.zeros((D,), dtype=jnp.float32)
        bk = jnp.zeros((D,), dtype=jnp.float32)
        bv = jnp.zeros((D,), dtype=jnp.float32)
        return {'x': x, 'Wq': Wq, 'bq': bq, 'Wk': Wk, 'bk': bk, 'Wv': Wv, 'bv': bv}
    _L0_attn_all = _L0_attn_setup()
    _L0_attn_in = {k: v for k, v in _L0_attn_all.items() if k in ('Wq', 'bq', 'Wk', 'bk', 'Wv', 'bv')}
    del _L0_attn_all

    def _L0_ffn_setup():
        import jax, jax.numpy as jnp
        import numpy as np
        B, S, D, E, H, K = (4, 1024, 64, 8, 128, 2)
        key = jax.random.key(seed)
        ks = jax.random.split(key, 6)
        x = jax.random.normal(ks[0], (B, S, D), jnp.float32)
        Wg = jax.random.normal(ks[1], (D, E), jnp.float32) * 0.02
        bg = jnp.zeros((E,), jnp.float32)
        W1 = jax.random.normal(ks[2], (E, D, H), jnp.float32) * 0.02
        b1 = jnp.zeros((E, H), jnp.float32)
        W2 = jax.random.normal(ks[3], (E, H, D), jnp.float32) * 0.02
        b2 = jnp.zeros((E, D), jnp.float32)
        return {'x': x, 'Wg': Wg, 'bg': bg, 'W1': W1, 'b1': b1, 'W2': W2, 'b2': b2}
    _L0_ffn_all = _L0_ffn_setup()
    _L0_ffn_in = {k: v for k, v in _L0_ffn_all.items() if k in ('Wg', 'bg', 'W1', 'b1', 'W2', 'b2')}
    del _L0_ffn_all
    return {'x': x, 'L0_tok_W': _L0_tok_in['W'], 'L0_attn_Wq': _L0_attn_in['Wq'], 'L0_attn_bq': _L0_attn_in['bq'], 'L0_attn_Wk': _L0_attn_in['Wk'], 'L0_attn_bk': _L0_attn_in['bk'], 'L0_attn_Wv': _L0_attn_in['Wv'], 'L0_attn_bv': _L0_attn_in['bv'], 'L0_ffn_Wg': _L0_ffn_in['Wg'], 'L0_ffn_bg': _L0_ffn_in['bg'], 'L0_ffn_W1': _L0_ffn_in['W1'], 'L0_ffn_b1': _L0_ffn_in['b1'], 'L0_ffn_W2': _L0_ffn_in['W2'], 'L0_ffn_b2': _L0_ffn_in['b2']}

def reference(x, L0_tok_W, L0_attn_Wq, L0_attn_bq, L0_attn_Wk, L0_attn_bk, L0_attn_Wv, L0_attn_bv, L0_ffn_Wg, L0_ffn_bg, L0_ffn_W1, L0_ffn_b1, L0_ffn_W2, L0_ffn_b2):
    import jax
    import jax.numpy as jnp

    def _L0_tok_ref(x, W):
        import jax, jax.numpy as jnp
        import numpy as np
        PATCH_LEN = 16
        STRIDE = 8
        PAD = 8
        B, C, T, V = x.shape
        xp = jnp.pad(x, ((0, 0), (0, 0), (0, PAD), (0, 0)), mode='edge')
        Tp = T + PAD
        N = (Tp - PATCH_LEN) // STRIDE + 1
        idx = jnp.arange(N)[:, None] * STRIDE + jnp.arange(PATCH_LEN)[None, :]
        patches = xp[:, :, idx, :]
        patches = jnp.transpose(patches, (0, 4, 2, 3, 1))
        xf = jnp.fft.rfft(patches, axis=-2, norm='ortho')
        F = xf.shape[-2]
        x_real = xf.real.reshape(B, V, N, F * C)
        x_imag = xf.imag.reshape(B, V, N, F * C)
        x_emb = jnp.concatenate([x_real, x_imag], axis=-1)
        x_emb = x_emb @ W.T
        return x_emb.reshape(B, V * N, -1)

    def _L0_attn_ref(x, Wq, bq, Wk, bk, Wv, bv):
        import jax, jax.numpy as jnp
        import numpy as np
        Q = jnp.einsum('bsd,de->bse', x, Wq) + bq
        K = jnp.einsum('bsd,de,->bse'.replace(',->', '->'), x, Wk) + bk
        V = jnp.einsum('bsd,de->bse', x, Wv) + bv
        scale = 1.0 / jnp.sqrt(jnp.asarray(Q.shape[-1], dtype=jnp.float32))
        scores = jnp.einsum('bqd,bkd->bqk', Q, K) * scale
        weights = jax.nn.softmax(scores, axis=-1)
        return jnp.einsum('bqk,bkd->bqd', weights, V)

    def _L0_ffn_ref(x, Wg, bg, W1, b1, W2, b2):
        import jax, jax.numpy as jnp
        import numpy as np
        B, S, D, E, H, K = (4, 1024, 64, 8, 128, 2)
        Bv, Sv, Dv = x.shape
        gate_scores = x @ Wg + bg
        _, idx = jax.lax.top_k(gate_scores, K)
        mask = jax.nn.one_hot(idx, E, dtype=x.dtype).sum(axis=-2)
        xf = x.reshape(-1, Dv)
        mf = mask.reshape(-1, E)
        h = jax.nn.gelu(jnp.einsum('td,edh->teh', xf, W1) + b1[None], approximate=False)
        y = jnp.einsum('teh,ehd->ted', h, W2) + b2[None]
        out = jnp.einsum('ted,te->td', y, mf)
        return out.reshape(Bv, Sv, Dv)
    h = _L0_tok_ref(x, L0_tok_W)
    h = _layernorm(h + _L0_attn_ref(h, L0_attn_Wq, L0_attn_bq, L0_attn_Wk, L0_attn_bk, L0_attn_Wv, L0_attn_bv), axis=-1)
    h = _layernorm(h + _L0_ffn_ref(h, L0_ffn_Wg, L0_ffn_bg, L0_ffn_W1, L0_ffn_b1, L0_ffn_W2, L0_ffn_b2), axis=-1)
    return h

_drawn_inputs = setup_inputs


def setup_inputs(seed=0):
    import zlib

    import numpy as np

    out = dict(_drawn_inputs(seed))
    spreads = {'L0_attn_bq': (0.0, 0.8),
     'L0_attn_bk': (0.0, 0.8),
     'L0_attn_bv': (0.0, 0.1),
     'L0_ffn_bg': (0.0, 0.1),
     'L0_ffn_b1': (0.0, 0.531),
     'L0_ffn_b2': (0.0, 0.1)}
    factors = {'L0_attn_Wq': 8.0, 'L0_attn_Wk': 8.0, 'L0_attn_Wv': 6.012}
    for name, (base, spread) in spreads.items():
        noise = np.random.default_rng([zlib.crc32(name.encode()), seed]).standard_normal(out[name].shape)
        drawn = base * np.exp(spread * noise) if base else spread * noise
        out[name] = jnp.asarray(drawn.astype(out[name].dtype))
    for name, factor in factors.items():
        out[name] = (out[name] * factor).astype(out[name].dtype)
    return out
```

```python
from contextlib import ExitStack

import numpy as np

import concourse.bass as bass
from concourse import mybir

F32 = mybir.dt.float32
F32R = mybir.dt.float32r
I32 = mybir.dt.int32
ALU = mybir.AluOpType
ACT = mybir.ActivationFunctionType
AX_X = mybir.AxisListType.X

P = 128
B, C, T, V = 2, 64, 128, 64
PATCH, STRIDE = 16, 8
NPATCH = T // STRIDE
NFREQ = PATCH // 2 + 1
NCOEF = 2 * NFREQ
D = 64
S = V * NPATCH
E, H = 8, 128
OI, O2 = 4, D // 4
TILES = S // P
NT = B * TILES
G = NT // 4
EPS = 1e-5
BIG = float(2.0 ** 60)
RSQRT_MAGIC = float(0x5F3759DF)
NEWTON = 3

PA_ID, PA_II, PA_WQ, PA_WK, PA_WV = 0, 128, 192, 320, 448
PA_BV, PA_BQ, PA_BK = 576, 704, 705
PA_WG, PA_BG, PA_LT, PA_N = 706, 714, 722, 786
PB_W1, PB_W1B, PB_W2, PB_B2, PB_N = 0, 1024, 2048, 2560, 2624
R_OFF, R_ONE, R_SEL, R_LOW = 64, 72, 73, 32


def vit_layer(nc, x, tok_pack, attn_pack, ffn_pack, out):
    with ExitStack() as ctx:
        def sb(name, shape, dt=F32):
            return ctx.enter_context(nc.sbuf_tensor(name, shape, dt))

        def sem(name):
            return ctx.enter_context(nc.semaphore(name))

        x_sb = sb("x_sb", [P, B, NPATCH, 4, V])
        tok_sb = sb("tok_sb", [OI * NCOEF, O2 * C + 72])
        attn_sb = sb("attn_sb", [P, PA_N])
        ffn_sb = sb("ffn_sb", [P, PB_N])
        tokw = sb("tokw", [P, 4, 2 * D])
        tokw_pad = sb("tokw_pad", [P, D])
        emb2 = sb("emb2", [P, B, TILES, V, 2])
        q_st = sb("q_st", [P, B, S], F32R)
        k_hi = sb("k_hi", [P, B, S], F32R)
        k_lo = sb("k_lo", [P, B, S], F32R)
        ve = sb("ve", [P, NT, 2 * D])
        prob = sb("prob", [P, 2, S])
        prob_t = sb("prob_t", [P, 2, TILES, 512])
        neg_max = sb("neg_max", [P, NT])
        row_sum = sb("row_sum", [P, NT])
        row_inv = sb("row_inv", [P, NT])
        ctx_t = sb("ctx_t", [P, 2, 512])
        res1 = sb("res1", [P, 2, 4, D])
        h1 = sb("h1", [P, NT, D])
        res2 = sb("res2", [P, 2, 4, D])
        fin = sb("fin", [P, G, 4, D])
        bst = sb("bst", [P, 2, 4, 6])
        mv = sb("mv", [P, 2, 4, 2])
        nw = sb("nw", [P, 2, 4, 4])
        bst2 = sb("bst2", [P, 4, 6])
        mv2 = sb("mv2", [P, 4, 2])
        nw2 = sb("nw2", [P, 4, 4])
        hl = sb("hl", [P, 2, 4, P])
        hm = sb("hm", [P, 2, 4, P])
        gate = sb("gate", [P, 2, 4, E])
        cmp_a = sb("cmp_a", [P, 4, E, E])
        cmp_b = sb("cmp_b", [P, 4, E, E])
        cmp_c = sb("cmp_c", [P, 4, E, E])
        rank = sb("rank", [P, 4, E])
        xs = sb("xs", [P, G, 512], F32R)
        xm = sb("xm", [P, G, 512], F32R)
        wg_hi = sb("wg_hi", [P, E], F32R)
        wg_lo = sb("wg_lo", [P, E], F32R)
        w1_hi = sb("w1_hi", [P, E, H], F32R)
        w1_lo = sb("w1_lo", [P, E, H], F32R)
        b2_r = sb("b2_r", [P, D], F32R)
        hid = sb("hid", [P, 2, 2, 512])
        ffn_t = sb("ffn_t", [P, 2, 512])

        bank = [ctx.enter_context(nc.psum_tensor(f"bank{i}", [P, 512], F32)) for i in range(4, 8)]
        quad = ctx.enter_context(nc.psum_tensor("quad", [P, 4, 512], F32))
        bank = [quad[:, i, :] for i in range(4)] + [t[:, :] for t in bank]
        PT_A, PT_B, PV, MISC = bank[4], bank[5], bank[6], bank[7]

        ld_tok = sem("ld_tok")
        ld_x = [sem(f"ld_x{i}") for i in range(4)]
        ld_attn = sem("ld_attn")
        ld_ffn = sem("ld_ffn")
        st_out = sem("st_out")
        wbuild = sem("wbuild")
        tokw_ready = sem("tokw_ready")
        tok_done = sem("tok_done")
        pad_done = sem("pad_done")
        emb_a = sem("emb_a")
        emb_b = sem("emb_b")
        proj = sem("proj")
        qk_act = sem("qk_act")
        qk_dve = sem("qk_dve")
        ve_ready = sem("ve_ready")
        scores = sem("scores")
        maxed = sem("maxed")
        expd = sem("expd")
        pt_a = sem("pt_a")
        pt_b = sem("pt_b")
        ptc_a = sem("ptc_a")
        ptc_b = sem("ptc_b")
        pv_done = sem("pv_done")
        ctx_ready = sem("ctx_ready")
        ctx_tok = sem("ctx_tok")
        res1_ready = sem("res1_ready")
        mv1 = sem("mv1")
        h_split = sem("h_split")
        hl_t = sem("hl_t")
        xs_ready = sem("xs_ready")
        gates = sem("gates")
        gates_sb = sem("gates_sb")
        hm_ready = sem("hm_ready")
        hm_t = sem("hm_t")
        xm_ready = sem("xm_ready")
        ffnw = sem("ffnw")
        consts = sem("consts")
        pre_done = sem("pre_done")
        hid_ready = sem("hid_ready")
        down_done = sem("down_done")
        ffn_ready = sem("ffn_ready")
        y_done = sem("y_done")
        fin_ready = sem("fin_ready")
        dchain = sem("dchain")
        pchain = sem("pchain")

        tok_w = tok_sb[:, 0:O2 * C].rearrange("p (o c) -> p o c", c=C)
        dft = tok_sb[:, O2 * C:O2 * C + 72].rearrange("p (q n) -> p q n", q=2)
        ident = attn_sb[:, PA_ID:PA_ID + P]
        twin = attn_sb[:, PA_II:PA_II + D]
        wq2 = attn_sb[:, PA_WQ:PA_WQ + P]
        wk2 = attn_sb[:, PA_WK:PA_WK + P]
        wv_i = attn_sb[:, PA_WV:PA_WV + P]
        bv_0 = attn_sb[:, PA_BV:PA_BV + P]
        bq = attn_sb[:, PA_BQ:PA_BQ + 1]
        bk = attn_sb[:, PA_BK:PA_BK + 1]
        wg2 = attn_sb[:, PA_WG:PA_WG + E]
        bg = attn_sb[:, PA_BG:PA_BG + E]
        before = attn_sb[:, PA_LT:PA_LT + E * E]
        w1_raw = ffn_sb[:, PB_W1:PB_W1 + E * H].rearrange("p (e h) -> p e h", e=E)
        w1b_raw = ffn_sb[:, PB_W1B:PB_W1B + E * H].rearrange("p (e h) -> p e h", e=E)
        w2 = ffn_sb[:, PB_W2:PB_W2 + E * D].rearrange("p (e d) -> p e d", e=E)
        b2_raw = ffn_sb[:, PB_B2:PB_B2 + D]

        wq_s = sb("wq_s", [P, P])
        bq_s = sb("bq_s", [P, 1])

        block = ctx.enter_context(nc.Block())

        @block.sync
        def _(sp):
            sp.dma_start(tok_sb[:, :], tok_pack).then_inc(ld_tok, 16)
            xv = x.rearrange("b c (m q r) v -> b q c m (r v)", q=2, r=4)
            for k in range(4):
                b, m = k // 2, 8 * (k % 2)
                for q in range(2):
                    sp.dma_start(x_sb[q * C:(q + 1) * C, b, m:m + 8, :, :].rearrange("c m r v -> c m (r v)"),
                                 xv[b, q, :, m:m + 8, :]).then_inc(ld_x[k], 16)
                if k == 1:
                    sp.dma_start(attn_sb[:, :], attn_pack).then_inc(ld_attn, 16)
            sp.dma_start(ffn_sb[:, :], ffn_pack).then_inc(ld_ffn, 16)
            ov = out.rearrange("b (p j) d -> b p j d", j=TILES)
            for g in range(G):
                sp.wait_ge(fin_ready, g + 1)
                sp.dma_start(ov[g // 2, :, 4 * (g % 2):4 * (g % 2) + 4, :], fin[:, g, :, :]).then_inc(st_out, 16)
            sp.wait_ge(st_out, 16 * G)

        @block.tensor
        def _(pe):
            pe.wait_ge(ld_tok, 16)
            for hb in range(2):
                for i in range(8):
                    for q in range(2):
                        last = nc.tensor.matmul(bank[hb][q * C:(q + 1) * C, 36 * i:36 * i + 36],
                                                tok_w[:, 8 * hb + i, :], dft[:, q, :], start=True, stop=True)
                last.then_inc(wbuild, 1)
            pe.wait_ge(tokw_ready, 4)

            def tokens(k, dst):
                b, m = k // 2, 8 * (k % 2)
                pe.wait_ge(ld_x[k], 32)
                for r in range(4):
                    last = nc.tensor.matmul(dst, tokw[:, r, :], x_sb[:, b, m:m + 8, r, :], start=(r == 0), stop=(r == 3))
                last.then_inc(tok_done, 1)
                if k % 2:
                    nc.tensor.matmul(MISC[C:P, 0:V], tokw_pad[:, :], x_sb[:, b, NPATCH - 1, 3, :],
                                     start=True, stop=True).then_inc(pad_done, 1)

            def project(b, order):
                pe.wait_ge(emb_a, 2 * (b + 1))
                pe.wait_ge(emb_b, 2 * (b + 1))
                e2 = emb2[:, b, :, :, :].rearrange("p j v n -> p (j v n)")
                for half in range(2):
                    for w, dst in ((wq_s, order[2 * half]), (wk2, order[2 * half + 1])):
                        nc.tensor.matmul(dst, w[:, :], e2[:, 512 * half:512 * half + 512],
                                         start=True, stop=True).then_inc(proj, 1)
                for half in range(2):
                    for i in range(4):
                        j = 4 * half + i
                        last = nc.tensor.matmul(order[4 + half][:, P * i:P * i + P], e2[:, P * j:P * j + P], wv_i,
                                                start=True, stop=True)
                    last.then_inc(proj, 1)

            def score(t):
                b, j = t // TILES, t % TILES
                for half in range(2):
                    ks = slice(512 * half, 512 * half + 512)
                    dst = quad[:, 2 * (t % 2) + half, :]
                    nc.tensor.matmul(dst, q_st[:, b, P * j:P * j + P], k_hi[:, b, ks], start=True, stop=False)
                    last = nc.tensor.matmul(dst, q_st[:, b, P * j:P * j + P], k_lo[:, b, ks], start=False, stop=True)
                last.then_inc(scores, 1)

            def turn(t):
                pe.wait_ge(expd, t + 1)
                if t >= 1:
                    pe.wait_ge(ptc_a, t)
                for kb in range(4):
                    last = nc.tensor.transpose(PT_A[:, P * kb:P * kb + P], prob[:, t % 2, P * kb:P * kb + P], ident)
                last.then_inc(pt_a, 1)
                if t >= 1:
                    pe.wait_ge(ptc_b, t)
                for kb in range(4):
                    last = nc.tensor.transpose(PT_B[:, P * kb:P * kb + P], prob[:, t % 2, 512 + P * kb:512 + P * kb + P], ident)
                last.then_inc(pt_b, 1)

            def weigh(g, i):
                if i == 0:
                    pe.wait_ge(ptc_a, 4 * g + 4)
                    pe.wait_ge(ptc_b, 4 * g + 4)
                    if g >= 1:
                        pe.wait_ge(ctx_ready, g)
                for half in range(2):
                    kb = 2 * i + half
                    last = nc.tensor.matmul(PV[half * D:(half + 1) * D, :], ve[:, (g // 2) * TILES + kb, 0:D],
                                            prob_t[:, g % 2, kb, :], start=(i == 0), stop=(i == 3))
                last.then_inc(pv_done, 1)

            def post(g, stage):
                if stage == 0:
                    pe.wait_ge(ctx_ready, g + 1)
                    if g >= 1:
                        pe.wait_ge(xm_ready, g)
                    for i in range(4):
                        last = nc.tensor.matmul(MISC[:, D * i:D * i + D], ctx_t[:, g % 2, P * i:P * i + P], twin,
                                                start=True, stop=True)
                    last.then_inc(ctx_tok, 1)
                if stage == 1:
                    pe.wait_ge(h_split, g + 1)
                    for i in range(4):
                        last = nc.tensor.transpose(MISC[:, P * i:P * i + P], hl[:, g % 2, i, :], ident)
                    last.then_inc(hl_t, 1)
                if stage == 2:
                    pe.wait_ge(xs_ready, g + 1)
                    for i in range(4):
                        dst = MISC[:, E * i:E * i + E]
                        nc.tensor.matmul(dst, xs[:, g, P * i:P * i + P], wg_hi[:, :], start=True, stop=False)
                        last = nc.tensor.matmul(dst, xs[:, g, P * i:P * i + P], wg_lo[:, :], start=False, stop=True)
                    last.then_inc(gates, 1)
                if stage == 3:
                    pe.wait_ge(hm_ready, g + 1)
                    for i in range(4):
                        last = nc.tensor.transpose(MISC[:, P * i:P * i + P], hm[:, g % 2, i, :], ident)
                    last.then_inc(hm_t, 1)

            tokens(0, bank[2])
            tokens(1, bank[3])
            pe.wait_ge(emb_a, 1)
            pe.wait_ge(emb_b, 1)
            tokens(2, bank[2])
            project(0, (bank[0], bank[1], bank[4], bank[5], bank[6], bank[3]))
            pe.wait_ge(ve_ready, 2)
            tokens(3, bank[3])
            pe.wait_ge(qk_dve, 4)
            score(0)
            project(1, (bank[4], bank[5], bank[6], bank[2], bank[3], bank[7]))
            pe.wait_ge(qk_dve, 8)
            pe.wait_ge(ve_ready, 4)
            score(1)
            for t in range(NT):
                turn(t)
                if t + 2 < NT:
                    score(t + 2)
                if t >= 4:
                    weigh((t - 4) // 4, t % 4)
                if t >= 8:
                    post((t - 8) // 4, t % 4)

            def up(u):
                g, i = u // 4, u % 4
                if i == 0:
                    pe.wait_ge(xm_ready, g + 1)
                if u >= 2:
                    pe.wait_ge(hid_ready, u - 1)
                for half in range(2):
                    e = 2 * i + half
                    dst = quad[:, 2 * (u % 2) + half, :]
                    nc.tensor.matmul(dst, w1_hi[:, e, :], xs[:, g, :], start=True, stop=False)
                    last = nc.tensor.matmul(dst, w1_lo[:, e, :], xm[:, g, :], start=False, stop=True)
                last.then_inc(pre_done, 1)

            def down(u):
                g, i = u // 4, u % 4
                pe.wait_ge(hid_ready, u + 1)
                if i == 0 and g >= 2:
                    pe.wait_ge(ffn_ready, g - 1)
                dst = (PT_A, PT_B)[g % 2]
                for half in range(2):
                    last = nc.tensor.matmul(dst[half * D:(half + 1) * D, :], w2[:, 2 * i + half, :], hid[:, u % 2, half, :],
                                            start=(i == 0), stop=(i == 3))
                last.then_inc(down_done, 1)

            def to_tokens(g):
                pe.wait_ge(ffn_ready, g + 1)
                if g >= 1:
                    pe.wait_ge(fin_ready, g)
                for i in range(4):
                    dst = PV[:, D * i:D * i + D]
                    nc.tensor.matmul(dst, ffn_t[:, g % 2, P * i:P * i + P], twin, start=True, stop=False)
                    last = nc.tensor.matmul(dst, xm[:, g, P * i:P * i + P], b2_r[:, :], start=False, stop=True)
                last.then_inc(y_done, 1)

            pe.wait_ge(ffnw, 1)
            pe.wait_ge(expd, NT)
            up(0)
            for u in range(NT):
                if u + 1 < NT:
                    up(u + 1)
                if u < 4:
                    weigh(3, u)
                if u < 8:
                    post(2 + u // 4, u % 4)
                down(u)
                if u >= 5 and u % 4 == 1:
                    to_tokens(u // 4 - 1)
            to_tokens(G - 1)

        @block.scalar
        def _(act):
            act.wait_ge(wbuild, 2)
            wv = bank[1][:, 0:288].rearrange("p (o i n) -> p i n o", i=OI, n=9)
            for half in range(2):
                dst = tokw[:, :, D * half:D * half + D].rearrange("p r (i o) -> p i r o", i=OI)[:, :, :, 8:16]
                nc.scalar.copy(dst, wv[:, :, 4 * half:4 * half + 4, :]).then_inc(tokw_ready, 1)
            nc.scalar.copy(tokw_pad[:, :].rearrange("p (i o) -> p i o", i=OI)[:, :, 8:16], wv[:, :, 8, :])\
                .then_inc(tokw_ready, 1)

            def emb(k):
                b, c = k // 2, k % 2
                act.wait_ge(tok_done, k + 1)
                src = (bank[2], bank[3])[c][0:C, :].rearrange("p (j v) -> p j v", v=V)
                ins = nc.scalar.copy(emb2[0:C, b, :, :, c], src)
                if c:
                    act.wait_ge(pad_done, b + 1)
                    ins = nc.scalar.copy(emb2[C:P, b, TILES - 1, :, 1], MISC[C:P, 0:V])
                ins.then_inc(emb_a, 1)

            def high_parts(b, order):
                for half in range(2):
                    for w, (dst, bias) in enumerate(((q_st, bq_s), (k_hi, bk))):
                        act.wait_ge(proj, 6 * b + 2 * half + w + 1)
                        nc.scalar.activation(dst[:, b, 512 * half:512 * half + 512], order[2 * half + w],
                                             ACT.Identity, bias=bias[:, 0:1]).then_inc(qk_act, 1)

            def softmax(t):
                act.wait_ge(maxed, t + 1)
                if t >= 2:
                    act.wait_ge(pt_b, t - 1)
                nc.scalar.activation(prob[:, t % 2, :], quad[:, 2 * (t % 2):2 * (t % 2) + 2, :].rearrange("p a n -> p (a n)"),
                                     ACT.Exp, bias=neg_max[:, t:t + 1], accum_out=row_sum[:, t:t + 1]).then_inc(expd, 1)

            def copy_turned(t):
                g = t // 4
                if g >= 2 and t % 4 == 0:
                    act.wait_ge(pv_done, 4 * (g - 1))
                act.wait_ge(pt_a, t + 1)
                nc.scalar.copy(prob_t[:, g % 2, 0:4, P * (t % 4):P * (t % 4) + P],
                               PT_A.rearrange("p (k n) -> p k n", n=P)).then_inc(ptc_a, 1)

            def ctx_copy(g):
                act.wait_ge(pv_done, 4 * g + 4)
                if g >= 2:
                    act.wait_ge(ctx_tok, g - 1)
                nc.scalar.copy(ctx_t[:, g % 2, :], PV).then_inc(ctx_ready, 1)

            def xs_copy(g):
                act.wait_ge(hl_t, g + 1)
                nc.scalar.copy(xs[:, g, :], MISC).then_inc(xs_ready, 1)

            def gelu(u):
                act.wait_ge(pre_done, u + 1)
                if u >= 2:
                    act.wait_ge(down_done, u - 1)
                nc.scalar.activation(hid[:, u % 2, :, :], quad[:, 2 * (u % 2):2 * (u % 2) + 2, :],
                                     ACT.Gelu).then_inc(hid_ready, 1)

            def ffn_copy(g):
                act.wait_ge(down_done, 4 * g + 4)
                if g >= 2:
                    act.wait_ge(y_done, g - 1)
                nc.scalar.copy(ffn_t[:, g % 2, :], (PT_A, PT_B)[g % 2]).then_inc(ffn_ready, 1)

            emb(0)
            emb(1)
            act.wait_ge(ld_attn, 16)
            emb(2)
            high_parts(0, (bank[0], bank[1], bank[4], bank[5]))
            emb(3)
            softmax(0)
            high_parts(1, (bank[4], bank[5], bank[6], bank[2]))
            for t in range(NT):
                if t + 1 < NT:
                    softmax(t + 1)
                copy_turned(t)
                if t >= 7 and t % 4 == 3:
                    ctx_copy(t // 4 - 1)
                if t >= 9 and t % 4 == 1:
                    xs_copy((t - 8) // 4)
            for u in range(NT):
                gelu(u)
                if u == 3:
                    ctx_copy(3)
                if u in (1, 5):
                    xs_copy(2 + u // 4)
                if u >= 4 and u % 4 == 0:
                    ffn_copy(u // 4 - 1)
            ffn_copy(G - 1)

        @block.vector
        def _(dve):
            chain = [0]

            def link(ins):
                chain[0] += 1
                ins.then_inc(dchain, 1)
                dve.wait_ge(dchain, chain[0])

            dve.wait_ge(wbuild, 1)
            wv = bank[0][:, 0:288].rearrange("p (o i n) -> p i n o", i=OI, n=9)
            for half in range(2):
                dst = tokw[:, :, D * half:D * half + D].rearrange("p r (i o) -> p i r o", i=OI)[:, :, :, 0:8]
                last = nc.vector.tensor_copy(dst, wv[:, :, 4 * half:4 * half + 4, :])
            last = nc.vector.tensor_copy(tokw_pad[:, :].rearrange("p (i o) -> p i o", i=OI)[:, :, 0:8], wv[:, :, 8, :])
            last.then_inc(tokw_ready, 1)

            def emb(k):
                b, c = k // 2, k % 2
                dve.wait_ge(tok_done, k + 1)
                src = (bank[2], bank[3])[c][C:P, :].rearrange("p (j v) -> p j v", v=V)
                if c:
                    nc.vector.tensor_copy(emb2[C:P, b, TILES - 1, :, 0], src[:, 0, :])
                nc.vector.tensor_copy(emb2[C:P, b, 0:TILES - 1, :, c], src[:, 1:TILES, :]).then_inc(emb_b, 1)

            def low_parts(b, order):
                for half in range(2):
                    sl = slice(512 * half, 512 * half + 512)
                    dve.wait_ge(qk_act, 4 * b + 2 * half + 1)
                    nc.vector.scalar_tensor_tensor(q_st[D:P, b, sl], order[2 * half][D:P, :], bq_s[D:P, 0:1],
                                                   q_st[D:P, b, sl].bitcast(F32), op0=ALU.add, op1=ALU.subtract)\
                        .then_inc(qk_dve, 1)
                    dve.wait_ge(qk_act, 4 * b + 2 * half + 2)
                    nc.vector.scalar_tensor_tensor(k_lo[:, b, sl], order[2 * half + 1], bk,
                                                   k_hi[:, b, sl].bitcast(F32), op0=ALU.add, op1=ALU.subtract)\
                        .then_inc(qk_dve, 1)

            def v_emb(b, order):
                for half in range(2):
                    dve.wait_ge(proj, 6 * b + 5 + half)
                    t0 = TILES * b + 4 * half
                    nc.vector.tensor_tensor(ve[:, t0:t0 + 4, :], order[4 + half].rearrange("p (i n) -> p i n", i=4),
                                            bv_0.unsqueeze(1).to_broadcast([P, 4, P]), ALU.add).then_inc(ve_ready, 1)

            def rowmax(t):
                dve.wait_ge(scores, t + 1)
                nc.vector.tensor_reduce(neg_max[:, t:t + 1],
                                        quad[:, 2 * (t % 2):2 * (t % 2) + 2, :].rearrange("p a n -> p (a n)"),
                                        axis=AX_X, op=ALU.max, negate=True).then_inc(maxed, 1)

            def copy_turned(t):
                g = t // 4
                if g >= 2 and t % 4 == 0:
                    dve.wait_ge(pv_done, 4 * (g - 1))
                dve.wait_ge(pt_b, t + 1)
                nc.vector.tensor_copy(prob_t[:, g % 2, 4:8, P * (t % 4):P * (t % 4) + P],
                                      PT_B.rearrange("p (k n) -> p k n", n=P)).then_inc(ptc_b, 1)

            def residual1(g):
                link(nc.vector.reciprocal(row_inv[:, 4 * g:4 * g + 4], row_sum[:, 4 * g:4 * g + 4]))
                dve.wait_ge(ctx_tok, g + 1)
                if g >= 2:
                    dve.wait_ge(h_split, g - 1)
                for i in range(4):
                    t = 4 * g + i
                    last = nc.vector.scalar_tensor_tensor(res1[:, g % 2, i, :], MISC[:, D * i:D * i + D], row_inv[:, t:t + 1],
                                                          ve[:, t, D:2 * D], op0=ALU.mult, op1=ALU.add)
                last.then_inc(res1_ready, 1)
                dve.wait_ge(res1_ready, g + 1)
                for i in range(4):
                    last = nc.vector.bn_stats(bst[:, g % 2, i, :], res1[:, g % 2, i, :])
                link(last)
                for i in range(4):
                    last = nc.vector.bn_aggr(mv[:, g % 2, i, :], bst[:, g % 2, i, :])
                last.then_inc(mv1, 1)

            def gate_bias(g):
                dve.wait_ge(gates, g + 1)
                if g >= 2:
                    dve.wait_ge(hm_ready, g - 1)
                nc.vector.tensor_tensor(gate[:, g % 2, :, :], MISC[:, 0:4 * E].rearrange("p (i e) -> p i e", e=E),
                                        bg.unsqueeze(1).to_broadcast([P, 4, E]), ALU.add).then_inc(gates_sb, 1)

            def xm_copy(g):
                dve.wait_ge(hm_t, g + 1)
                nc.vector.tensor_copy(xm[:, g, :], MISC).then_inc(xm_ready, 1)

            def norm2(g):
                dve.wait_ge(y_done, g + 1)
                link(nc.vector.tensor_tensor(res2[:, g % 2, :, :], PV[:, 0:4 * D].rearrange("p (i d) -> p i d", d=D),
                                             h1[:, 4 * g:4 * g + 4, :], ALU.add))
                for i in range(4):
                    last = nc.vector.bn_stats(bst2[:, i, :], res2[:, g % 2, i, :])
                link(last)
                for i in range(4):
                    last = nc.vector.bn_aggr(mv2[:, i, :], bst2[:, i, :])
                link(last)
                a, y, z = nw2[:, :, 0], nw2[:, :, 1], nw2[:, :, 2]
                link(nc.vector.tensor_scalar(a, mv2[:, :, 1], EPS, None, ALU.add))
                link(nc.vector.tensor_scalar(y.bitcast(I32), a.bitcast(I32), -0.5, RSQRT_MAGIC, ALU.mult, ALU.add))
                for _ in range(NEWTON):
                    link(nc.vector.scalar_tensor_tensor(z, y, -0.5, y, op0=ALU.mult, op1=ALU.mult))
                    link(nc.vector.tensor_tensor(z, z, a, ALU.mult))
                    link(nc.vector.scalar_tensor_tensor(y, z, 1.5, y, op0=ALU.add, op1=ALU.mult))
                for i in range(4):
                    last = nc.vector.tensor_scalar(fin[:, g, i, :], res2[:, g % 2, i, :], mv2[:, i, 0:1], nw2[:, i, 1:2],
                                                   ALU.subtract, ALU.mult)
                last.then_inc(fin_ready, 1)

            dve.wait_ge(ld_attn, 16)
            nc.vector.tensor_scalar(wq_s[:, :], wq2, D ** -0.5, None, ALU.mult)
            link(nc.vector.tensor_scalar(bq_s[:, :], bq, D ** -0.5, None, ALU.mult))
            emb(0)
            emb(1)
            emb(2)
            low_parts(0, (bank[0], bank[1], bank[4], bank[5]))
            v_emb(0, (bank[0], bank[1], bank[4], bank[5], bank[6], bank[3]))
            emb(3)
            rowmax(0)
            low_parts(1, (bank[4], bank[5], bank[6], bank[2]))
            v_emb(1, (bank[4], bank[5], bank[6], bank[2], bank[3], bank[7]))
            rowmax(1)
            for t in range(NT):
                copy_turned(t)
                if t + 2 < NT:
                    rowmax(t + 2)
                if t >= 8:
                    g = (t - 8) // 4
                    if t % 4 == 0:
                        residual1(g)
                    if t % 4 == 2:
                        gate_bias(g)
                    if t % 4 == 3:
                        xm_copy(g)
            for u in range(8):
                g = 2 + u // 4
                if u % 4 == 0:
                    residual1(g)
                if u % 4 == 2:
                    gate_bias(g)
                if u % 4 == 3:
                    xm_copy(g)
                if u == 6:
                    norm2(0)
            for g in range(1, G):
                norm2(g)

        @block.gpsimd
        def _(pool):
            chain = [0]

            def link(ins):
                chain[0] += 1
                ins.then_inc(pchain, 1)
                pool.wait_ge(pchain, chain[0])

            link(nc.gpsimd.memset(hm[:, :, :, D:P], 0.0))
            hm_lo = hm[:, :, :, D:P].rearrange("p a i (z n) -> p a i z n", n=R_LOW)
            for a in range(2):
                nc.gpsimd.memset(hm_lo[:, a, :, :, R_ONE - D], 1.0)
            pool.wait_ge(ld_attn, 16)
            link(nc.gpsimd.tensor_copy(wg_hi[:, :], wg2))
            link(nc.gpsimd.tensor_tensor(wg_lo[:, :], wg2, wg_hi[:, :].bitcast(F32), ALU.subtract))
            pool.wait_ge(ld_ffn, 16)
            link(nc.gpsimd.tensor_copy(b2_r[:, :], b2_raw))
            link(nc.gpsimd.tensor_copy(w1_lo[D:P, :, :], w1b_raw[D:P, :, :]))
            link(nc.gpsimd.tensor_copy(w1_hi[:, :, :], w1_raw))
            link(nc.gpsimd.tensor_tensor(b2_r[96:P, :], b2_raw[96:P, :], b2_r[96:P, :].bitcast(F32), ALU.subtract))
            link(nc.gpsimd.tensor_tensor(w1_lo[96:P, :, :], w1b_raw[96:P, :, :], w1_lo[96:P, :, :].bitcast(F32), ALU.subtract))
            nc.gpsimd.tensor_tensor(w1_lo[0:D, :, :], w1b_raw[0:D, :, :], w1_hi[0:D, :, :].bitcast(F32), ALU.subtract)\
                .then_inc(ffnw, 1)
            pool.wait_ge(ffnw, 1)

            for g in range(G):
                s = g % 2
                pool.wait_ge(mv1, g + 1)
                a, y, z = nw[:, s, :, 0], nw[:, s, :, 1], nw[:, s, :, 2]
                link(nc.gpsimd.tensor_scalar(a, mv[:, s, :, 1], EPS, None, ALU.add))
                link(nc.gpsimd.tensor_scalar(y.bitcast(I32), a.bitcast(I32), -0.5, RSQRT_MAGIC, ALU.mult, ALU.add))
                link(nc.gpsimd.tensor_scalar(a, a, -0.5, None, ALU.mult))
                for _ in range(NEWTON):
                    link(nc.gpsimd.tensor_tensor(z, y, y, ALU.mult))
                    link(nc.gpsimd.tensor_tensor(z, z, a, ALU.mult))
                    link(nc.gpsimd.tensor_scalar(z, z, 1.5, None, ALU.add))
                    link(nc.gpsimd.tensor_tensor(y, z, y, ALU.mult))
                for i in range(4):
                    last = nc.gpsimd.tensor_scalar(h1[:, 4 * g + i, :], res1[:, s, i, :], mv[:, s, i, 0:1], nw[:, s, i, 1:2],
                                                   ALU.subtract, ALU.mult)
                link(last)
                if g >= 2:
                    pool.wait_ge(hm_t, g - 1)
                hv = h1[:, 4 * g:4 * g + 4, :]
                nc.gpsimd.tensor_copy(hm[:, s, :, 0:D].bitcast(F32R), hv)
                link(nc.gpsimd.tensor_copy(hl[:, s, :, 0:D].bitcast(F32R), hv))
                nc.gpsimd.tensor_tensor(hl[:, s, :, D:P], hv, hl[:, s, :, 0:D], ALU.subtract).then_inc(h_split, 1)
                pool.wait_ge(gates_sb, g + 1)
                sj = gate[:, s, :, :].unsqueeze(2).to_broadcast([P, 4, E, E])
                se = gate[:, s, :, :].unsqueeze(3).to_broadcast([P, 4, E, E])
                lt = before.rearrange("p (e j) -> p e j", e=E).unsqueeze(1).to_broadcast([P, 4, E, E])
                link(nc.gpsimd.tensor_tensor(cmp_c[:, :, :, :], sj, se, ALU.subtract))
                nc.gpsimd.tensor_scalar(cmp_a[:, :, :, :], cmp_c[:, :, :, :], 0.0, None, ALU.is_gt)
                link(nc.gpsimd.tensor_scalar(cmp_b[:, :, :, :], cmp_c[:, :, :, :], 0.0, None, ALU.is_equal))
                link(nc.gpsimd.tensor_tensor(cmp_c[:, :, :, :], cmp_b[:, :, :, :], lt, ALU.mult))
                link(nc.gpsimd.tensor_tensor(cmp_b[:, :, :, :], cmp_a[:, :, :, :], cmp_c[:, :, :, :], ALU.add))
                link(nc.gpsimd.tensor_tensor(cmp_a[:, :, :, 0:4], cmp_b[:, :, :, 0:4], cmp_b[:, :, :, 4:8], ALU.add))
                link(nc.gpsimd.tensor_tensor(cmp_c[:, :, :, 0:2], cmp_a[:, :, :, 0:2], cmp_a[:, :, :, 2:4], ALU.add))
                link(nc.gpsimd.tensor_tensor(rank[:, :, :], cmp_c[:, :, :, 0], cmp_c[:, :, :, 1], ALU.add))
                nc.gpsimd.tensor_scalar(hm[:, s, :, R_SEL:R_SEL + E], rank[:, :, :], 1.5, None, ALU.is_lt)
                nc.gpsimd.tensor_scalar(hm[:, s, :, R_LOW + R_SEL:R_LOW + R_SEL + E], rank[:, :, :], 1.5, None, ALU.is_lt)
                nc.gpsimd.tensor_scalar(hm[:, s, :, R_OFF:R_OFF + E], rank[:, :, :], 1.5, None, ALU.is_gt).then_inc(hm_ready, 1)


def dft_columns():
    k, p = np.arange(NFREQ)[:, None], np.arange(PATCH)[None, :]
    angle = 2 * np.pi * k * p / PATCH
    coef = np.concatenate([np.cos(angle), -np.sin(angle)], 0) / np.sqrt(PATCH)
    cols = np.zeros((OI, NCOEF, 2, OI, 9))
    for i in range(OI):
        for q in range(2):
            for h in range(2):
                cols[i, :, q, i, 4 * h:4 * h + 4] = coef[:, 8 * h + 4 * q:8 * h + 4 * q + 4]
        cols[i, :, 1, i, 8] = coef[:, 8:16].sum(1)
    return cols.reshape(OI * NCOEF, 2 * OI * 9).astype(np.float32)


def kernel(**inputs):
    import concourse.bacc as bacc
    from concourse.bass_utils import run_bass_kernel_spmd

    a = {n.removeprefix("L0_"): np.ascontiguousarray(v) for n, v in inputs.items()}
    f4 = np.float32
    w = a["tok_W"].reshape(OI, O2, NCOEF, C).transpose(0, 2, 1, 3).reshape(OI * NCOEF, O2 * C)
    tok_pack = np.concatenate([w, dft_columns()], 1)

    eye = np.eye(D, dtype=f4)
    before = np.tile(np.tril(np.ones((E, E), f4), -1).reshape(1, E * E), (P, 1))
    two = lambda m: np.concatenate([m, m], 0)
    rows = lambda m: np.tile(m.reshape(1, -1), (P, 1))
    attn_pack = np.zeros((P, PA_N), f4)
    attn_pack[:, PA_ID:PA_ID + P] = np.eye(P, dtype=f4)
    attn_pack[:, PA_II:PA_II + D] = two(eye)
    for at, m in ((PA_WQ, a["attn_Wq"]), (PA_WK, a["attn_Wk"])):
        attn_pack[:, at:at + P] = np.concatenate([two(m), two(m)], 1)
    attn_pack[:, PA_WV:PA_WV + P] = np.concatenate([two(a["attn_Wv"]), two(eye)], 1)
    attn_pack[:, PA_BV:PA_BV + D] = rows(a["attn_bv"])
    attn_pack[:, PA_BQ] = two(a["attn_bq"])
    attn_pack[:, PA_BK] = two(a["attn_bk"])
    attn_pack[:, PA_WG:PA_WG + E] = two(a["ffn_Wg"])
    attn_pack[:, PA_BG:PA_BG + E] = rows(a["ffn_bg"])
    attn_pack[:, PA_LT:PA_LT + E * E] = before

    ffn_pack = np.zeros((P, PB_N), f4)
    w1 = a["ffn_W1"].transpose(1, 0, 2).reshape(D, E * H)
    ffn_pack[:, PB_W1:PB_W1 + E * H] = two(w1)
    ffn_pack[0:D, PB_W1B:PB_W1B + E * H] = w1
    off = np.zeros((E, E, H), f4)
    off[np.arange(E), np.arange(E), :] = -BIG
    for low in (0, R_LOW):
        ffn_pack[R_OFF + low:R_OFF + low + E, PB_W1B:PB_W1B + E * H] = off.reshape(E, E * H)
        ffn_pack[R_ONE + low, PB_W1B:PB_W1B + E * H] = a["ffn_b1"].reshape(-1)
        ffn_pack[R_SEL + low:R_SEL + low + E, PB_B2:PB_B2 + D] = a["ffn_b2"]
    ffn_pack[:, PB_W2:PB_W2 + E * D] = a["ffn_W2"].transpose(1, 0, 2).reshape(H, E * D)

    nc = bacc.Bacc("TRN2", target_bir_lowering=False, num_devices=1)
    arrays = {"x_dram": a["x"], "tok_pack": tok_pack, "attn_pack": attn_pack, "ffn_pack": ffn_pack}
    args = [nc.dram_tensor(n, v.shape, F32, kind="ExternalInput").ap() for n, v in arrays.items()]
    args.append(nc.dram_tensor("out_dram", (B, S, D), F32, kind="ExternalOutput").ap())
    vit_layer(nc, *args)
    r = run_bass_kernel_spmd(nc, [arrays], core_ids=[0])
    return r.results[0]["out_dram"]
```

```python
from contextlib import ExitStack

import numpy as np

import concourse.bass as bass
from concourse import mybir

F32 = mybir.dt.float32
F32R = mybir.dt.float32r
I32 = mybir.dt.int32
ALU = mybir.AluOpType
ACT = mybir.ActivationFunctionType
AX_X = mybir.AxisListType.X

P = 128
B, C, T, V = 2, 64, 128, 64
PATCH, STRIDE = 16, 8
NPATCH = T // STRIDE
NFREQ = PATCH // 2 + 1
NCOEF = 2 * NFREQ
D = 64
S = V * NPATCH
E, H = 8, 128
OI, O2 = 4, D // 4
TILES = S // P
NT = B * TILES
G = NT // 4
EPS = 1e-5
BIG = float(2.0 ** 60)
RSQRT_MAGIC = float(0x5F3759DF)
NEWTON = 3

PA_ID, PA_II, PA_WQ, PA_WK, PA_WV = 0, 128, 192, 320, 448
PA_BV, PA_BQ, PA_BK = 576, 704, 705
PA_WG, PA_BG, PA_LT, PA_N = 706, 714, 722, 786
PB_W1, PB_W1B, PB_W2, PB_B2, PB_N = 0, 1024, 2048, 2560, 2624
R_OFF, R_ONE, R_SEL, R_LOW = 64, 72, 73, 32

TOK_BANK = (2, 3, 0, 1)
PAD_BANK = (7, 6)
STEPS = 2 * NT
POST_PE = ((8, 0), (10, 1), (11, 2), (13, 3))
FFN_OUT = NT + 5


def vit_layer(nc, x, tok_pack, attn_pack, ffn_pack, out):
    with ExitStack() as ctx:
        def sb(name, shape, dt=F32):
            return ctx.enter_context(nc.sbuf_tensor(name, shape, dt))

        def sem(name):
            return ctx.enter_context(nc.semaphore(name))

        x_sb = sb("x_sb", [P, B, NPATCH, 4, V])
        tok_sb = sb("tok_sb", [OI * NCOEF, O2 * C + 72])
        attn_sb = sb("attn_sb", [P, PA_N])
        ffn_sb = sb("ffn_sb", [P, PB_N])
        tokw = sb("tokw", [P, 4, 2 * D])
        tokw_pad = sb("tokw_pad", [P, D])
        emb2 = sb("emb2", [P, B, TILES, V, 2])
        q_st = sb("q_st", [P, B, S], F32R)
        k_hi = sb("k_hi", [P, B, S], F32R)
        k_lo = sb("k_lo", [P, B, S], F32R)
        ve = sb("ve", [P, NT, 2 * D])
        prob = sb("prob", [P, 2, S])
        prob_t = sb("prob_t", [P, 2, TILES, 512])
        neg_max = sb("neg_max", [P, NT])
        row_sum = sb("row_sum", [P, NT])
        row_inv = sb("row_inv", [P, NT])
        ctx_t = sb("ctx_t", [P, 2, 512])
        res1 = sb("res1", [P, 4, D])
        h1 = sb("h1", [P, NT, D])
        res2 = sb("res2", [P, 4, D])
        fin = sb("fin", [P, G, 4, D])
        bst = sb("bst", [P, 4, 6])
        mv = sb("mv", [P, 4, 2])
        nw = sb("nw", [P, 4, 4])
        hl = sb("hl", [P, 2, 4, P])
        hm = sb("hm", [P, 2, 4, P])
        gate = sb("gate", [P, 4, E])
        ahead = sb("ahead", [P, 4, E, E])
        tied = sb("tied", [P, 4, E * E])
        beaten = sb("beaten", [P, 4, E * E])
        rank = sb("rank", [P, 4, E])
        xs = sb("xs", [P, G, 512], F32R)
        xm = sb("xm", [P, G, 512], F32R)
        wg_hi = sb("wg_hi", [P, E], F32R)
        wg_lo = sb("wg_lo", [P, E], F32R)
        w1_hi = sb("w1_hi", [P, E, H], F32R)
        w1_lo = sb("w1_lo", [P, E, H], F32R)
        b2_r = sb("b2_r", [P, D], F32R)
        hid = sb("hid", [P, 2, 2, 512])
        ffn_t = sb("ffn_t", [P, 2, 512])

        ps = ctx.enter_context(nc.psum_tensor("ps", [P, 8, 512], F32))
        bank = [ps[:, i, :] for i in range(8)]
        quad = ps[:, 0:4, :]
        turned = ps[:, 4:6, :]
        proj_banks = ((4, 5, 2, 3, 7, 4), (5, 6, 7, 4, 5, 6))
        PV, MISC = bank[6], bank[7]
        DOWN = (bank[4], bank[5])

        ld_tok = sem("ld_tok")
        ld_x = [sem(f"ld_x{i}") for i in range(4)]
        ld_attn = sem("ld_attn")
        ld_ffn = sem("ld_ffn")
        st_out = sem("st_out")
        wbuild = sem("wbuild")
        tokw_ready = sem("tokw_ready")
        tok_done = sem("tok_done")
        pad_done = sem("pad_done")
        emb_a = sem("emb_a")
        emb_b = sem("emb_b")
        proj_qk = sem("proj_qk")
        proj_v = sem("proj_v")
        scaled = sem("scaled")
        res2_ready = sem("res2_ready")
        qk_act = sem("qk_act")
        qk_dve = sem("qk_dve")
        ve_ready = sem("ve_ready")
        scores = sem("scores")
        maxed = sem("maxed")
        expd = sem("expd")
        pt_done = sem("pt_done")
        pt_ready = sem("pt_ready")
        pv_done = sem("pv_done")
        ctx_ready = sem("ctx_ready")
        ctx_tok = sem("ctx_tok")
        res1_ready = sem("res1_ready")
        h_high = sem("h_high")
        h1_ready = sem("h1_ready")
        h_split = sem("h_split")
        hl_t = sem("hl_t")
        xs_ready = sem("xs_ready")
        gates = sem("gates")
        mask_ready = sem("mask_ready")
        hm_t = sem("hm_t")
        xm_ready = sem("xm_ready")
        ffnw = sem("ffnw")
        consts = sem("consts")
        pre_done = sem("pre_done")
        hid_ready = sem("hid_ready")
        down_done = sem("down_done")
        ffn_ready = sem("ffn_ready")
        y_done = sem("y_done")
        fin_ready = sem("fin_ready")
        dchain = sem("dchain")
        pchain = sem("pchain")

        tok_w = tok_sb[:, 0:O2 * C].rearrange("p (o c) -> p o c", c=C)
        dft = tok_sb[:, O2 * C:O2 * C + 72].rearrange("p (q n) -> p q n", q=2)
        ident = attn_sb[:, PA_ID:PA_ID + P]
        twin = attn_sb[:, PA_II:PA_II + D]
        wq2 = attn_sb[:, PA_WQ:PA_WQ + P]
        wk2 = attn_sb[:, PA_WK:PA_WK + P]
        wv_i = attn_sb[:, PA_WV:PA_WV + P]
        bv_0 = attn_sb[:, PA_BV:PA_BV + P]
        bq = attn_sb[:, PA_BQ:PA_BQ + 1]
        bk = attn_sb[:, PA_BK:PA_BK + 1]
        wg2 = attn_sb[:, PA_WG:PA_WG + E]
        bg = attn_sb[:, PA_BG:PA_BG + E]
        before = attn_sb[:, PA_LT:PA_LT + E * E]
        w1_raw = ffn_sb[:, PB_W1:PB_W1 + E * H].rearrange("p (e h) -> p e h", e=E)
        w1b_raw = ffn_sb[:, PB_W1B:PB_W1B + E * H].rearrange("p (e h) -> p e h", e=E)
        w2 = ffn_sb[:, PB_W2:PB_W2 + E * D].rearrange("p (e d) -> p e d", e=E)
        b2_raw = ffn_sb[:, PB_B2:PB_B2 + D]

        wq_s = sb("wq_s", [P, P])
        bq_s = sb("bq_s", [P, 1])

        block = ctx.enter_context(nc.Block())

        @block.sync
        def _(sp):
            sp.dma_start(tok_sb[:, :], tok_pack).then_inc(ld_tok, 16)
            xv = x.rearrange("b c (m q r) v -> b q c m (r v)", q=2, r=4)
            for k in range(4):
                b, m = k // 2, 8 * (k % 2)
                for q in range(2):
                    sp.dma_start(x_sb[q * C:(q + 1) * C, b, m:m + 8, :, :].rearrange("c m r v -> c m (r v)"),
                                 xv[b, q, :, m:m + 8, :]).then_inc(ld_x[k], 16)
                if k == 1:
                    sp.dma_start(attn_sb[:, :], attn_pack).then_inc(ld_attn, 16)
            sp.dma_start(ffn_sb[:, :], ffn_pack).then_inc(ld_ffn, 16)
            ov = out.rearrange("b (p j) d -> b p j d", j=TILES)
            for g in range(G):
                sp.wait_ge(fin_ready, g + 1)
                sp.dma_start(ov[g // 2, :, 4 * (g % 2):4 * (g % 2) + 4, :], fin[:, g, :, :]).then_inc(st_out, 16)
            sp.wait_ge(st_out, 16 * G)

        @block.tensor
        def _(pe):
            pe.wait_ge(ld_tok, 16)
            for hb in range(2):
                for i in range(8):
                    for q in range(2):
                        last = nc.tensor.matmul(bank[hb][q * C:(q + 1) * C, 36 * i:36 * i + 36],
                                                tok_w[:, 8 * hb + i, :], dft[:, q, :], start=True, stop=True)
                last.then_inc(wbuild, 1)
            pe.wait_ge(tokw_ready, 4)

            def tokens(k):
                b, m, dst = k // 2, 8 * (k % 2), bank[TOK_BANK[k]]
                pe.wait_ge(ld_x[k], 32)
                for r in range(4):
                    last = nc.tensor.matmul(dst, tokw[:, r, :], x_sb[:, b, m:m + 8, r, :], start=(r == 0), stop=(r == 3))
                last.then_inc(tok_done, 1)
                if k % 2:
                    nc.tensor.matmul(bank[PAD_BANK[b]][C:P, 0:V], tokw_pad[:, :], x_sb[:, b, NPATCH - 1, 3, :],
                                     start=True, stop=True).then_inc(pad_done, 1)

            def project_qk(b):
                pe.wait_ge(emb_a, 2 * (b + 1))
                pe.wait_ge(emb_b, 2 * (b + 1))
                e2 = emb2[:, b, :, :, :].rearrange("p j v n -> p (j v n)")
                for half in range(2):
                    for i, w in enumerate((wq_s, wk2)):
                        nc.tensor.matmul(bank[proj_banks[b][2 * half + i]], w[:, :], e2[:, 512 * half:512 * half + 512],
                                         start=True, stop=True).then_inc(proj_qk, 1)

            def project_v(b, half):
                e2 = emb2[:, b, :, :, :].rearrange("p j v n -> p (j v n)")
                for i in range(4):
                    j = 4 * half + i
                    last = nc.tensor.matmul(bank[proj_banks[b][4 + half]][:, P * i:P * i + P], e2[:, P * j:P * j + P], wv_i,
                                            start=True, stop=True)
                last.then_inc(proj_v, 1)

            def score(t):
                b, j = t // TILES, t % TILES
                for half in range(2):
                    ks = slice(512 * half, 512 * half + 512)
                    dst = quad[:, 2 * (t % 2) + half, :]
                    nc.tensor.matmul(dst, q_st[:, b, P * j:P * j + P], k_hi[:, b, ks], start=True, stop=False)
                    last = nc.tensor.matmul(dst, q_st[:, b, P * j:P * j + P], k_lo[:, b, ks], start=False, stop=True)
                last.then_inc(scores, 1)

            def turn(t):
                pe.wait_ge(expd, t + 1)
                if t >= 1:
                    pe.wait_ge(pt_ready, t)
                for kb in range(TILES):
                    last = nc.tensor.transpose(turned[:, kb // 4, P * (kb % 4):P * (kb % 4) + P],
                                               prob[:, t % 2, P * kb:P * kb + P], ident)
                last.then_inc(pt_done, 1)

            def weigh(g, i):
                if i == 0:
                    pe.wait_ge(pt_ready, 4 * g + 4)
                    if g >= 1:
                        pe.wait_ge(ctx_ready, g)
                for half in range(2):
                    kb = 2 * i + half
                    last = nc.tensor.matmul(PV[half * D:(half + 1) * D, :], ve[:, (g // 2) * TILES + kb, 0:D],
                                            prob_t[:, g % 2, kb, :], start=(i == 0), stop=(i == 3))
                last.then_inc(pv_done, 1)

            def ctx_to_tokens(g):
                pe.wait_ge(ctx_ready, g + 1)
                if g >= 1:
                    pe.wait_ge(mask_ready, g)
                for i in range(4):
                    last = nc.tensor.matmul(MISC[:, D * i:D * i + D], ctx_t[:, g % 2, P * i:P * i + P], twin,
                                            start=True, stop=True)
                last.then_inc(ctx_tok, 1)

            def turn_x(g):
                pe.wait_ge(h_split, g + 1)
                if g >= 1:
                    pe.wait_ge(xm_ready, g)
                for i in range(4):
                    last = nc.tensor.transpose(MISC[:, P * i:P * i + P], hl[:, g % 2, i, :], ident)
                last.then_inc(hl_t, 1)

            def gate_scores(g):
                pe.wait_ge(xs_ready, g + 1)
                if g == 0:
                    pe.wait_ge(consts, 1)
                for i in range(4):
                    dst = MISC[:, E * i:E * i + E]
                    nc.tensor.matmul(dst, xs[:, g, P * i:P * i + P], wg_hi[:, :], start=True, stop=False)
                    last = nc.tensor.matmul(dst, xs[:, g, P * i:P * i + P], wg_lo[:, :], start=False, stop=True)
                last.then_inc(gates, 1)

            def turn_flags(g):
                pe.wait_ge(mask_ready, g + 1)
                pe.wait_ge(h_high, g + 1)
                if g + 1 < G:
                    pe.wait_ge(res1_ready, g + 2)
                for i in range(4):
                    last = nc.tensor.transpose(MISC[:, P * i:P * i + P], hm[:, g % 2, i, :], ident)
                last.then_inc(hm_t, 1)

            def up(u):
                g, i = u // 4, u % 4
                if i == 0:
                    pe.wait_ge(xm_ready, g + 1)
                if u >= 2:
                    pe.wait_ge(hid_ready, u - 1)
                for half in range(2):
                    e = 2 * i + half
                    dst = quad[:, 2 * (u % 2) + half, :]
                    nc.tensor.matmul(dst, w1_hi[:, e, :], xs[:, g, :], start=True, stop=False)
                    last = nc.tensor.matmul(dst, w1_lo[:, e, :], xm[:, g, :], start=False, stop=True)
                last.then_inc(pre_done, 1)

            def down(u):
                g, i = u // 4, u % 4
                pe.wait_ge(hid_ready, u + 1)
                if i == 0 and g >= 2:
                    pe.wait_ge(ffn_ready, g - 1)
                dst = DOWN[g % 2]
                for half in range(2):
                    last = nc.tensor.matmul(dst[half * D:(half + 1) * D, :], w2[:, 2 * i + half, :], hid[:, u % 2, half, :],
                                            start=(i == 0), stop=(i == 3))
                last.then_inc(down_done, 1)

            def ffn_to_tokens(g):
                pe.wait_ge(ffn_ready, g + 1)
                if g >= 1:
                    pe.wait_ge(res2_ready, g)
                for i in range(4):
                    dst = PV[:, D * i:D * i + D]
                    nc.tensor.matmul(dst, ffn_t[:, g % 2, P * i:P * i + P], twin, start=True, stop=False)
                    last = nc.tensor.matmul(dst, xm[:, g, P * i:P * i + P], b2_r[:, :], start=False, stop=True)
                last.then_inc(y_done, 1)

            tokens(0)
            tokens(1)
            tokens(2)
            project_qk(0)
            project_v(0, 0)
            tokens(3)
            pe.wait_ge(qk_dve, 1)
            project_v(0, 1)
            pe.wait_ge(qk_dve, 4)
            pe.wait_ge(emb_a, 4)
            pe.wait_ge(emb_b, 4)
            score(0)
            score(1)
            pe.wait_ge(ve_ready, 2)
            project_qk(1)
            pe.wait_ge(qk_dve, 6)
            project_v(1, 0)
            project_v(1, 1)
            for step in range(STEPS):
                if step < NT:
                    if step == 0:
                        pe.wait_ge(qk_dve, 8)
                        pe.wait_ge(ve_ready, 4)
                    turn(step)
                    if step + 2 < NT:
                        score(step + 2)
                else:
                    u = step - NT
                    if u == 0:
                        pe.wait_ge(ffnw, 1)
                        up(0)
                    if u + 1 < NT:
                        up(u + 1)
                for g in range(G):
                    if 4 * g + 4 <= step < 4 * g + 8:
                        weigh(g, step % 4)
                    for at, stage in POST_PE:
                        if step == 4 * g + at:
                            (ctx_to_tokens, turn_x, gate_scores, turn_flags)[stage](g)
                if step >= NT:
                    down(step - NT)
                for g in range(G - 1):
                    if step == FFN_OUT + 4 * g:
                        ffn_to_tokens(g)
            ffn_to_tokens(G - 1)

        @block.scalar
        def _(act):
            act.wait_ge(wbuild, 2)
            wv = bank[1][:, 0:288].rearrange("p (o i n) -> p i n o", i=OI, n=9)
            for half in range(2):
                dst = tokw[:, :, D * half:D * half + D].rearrange("p r (i o) -> p i r o", i=OI)[:, :, :, 8:16]
                nc.scalar.copy(dst, wv[:, :, 4 * half:4 * half + 4, :]).then_inc(tokw_ready, 1)
            nc.scalar.copy(tokw_pad[:, :].rearrange("p (i o) -> p i o", i=OI)[:, :, 8:16], wv[:, :, 8, :])\
                .then_inc(tokw_ready, 1)

            def emb(k):
                b, c = k // 2, k % 2
                act.wait_ge(tok_done, k + 1)
                src = bank[TOK_BANK[k]][0:C, :].rearrange("p (j v) -> p j v", v=V)
                ins = nc.scalar.copy(emb2[0:C, b, :, :, c], src)
                if c:
                    act.wait_ge(pad_done, b + 1)
                    ins = nc.scalar.copy(emb2[C:P, b, TILES - 1, :, 1], bank[PAD_BANK[b]][C:P, 0:V])
                ins.then_inc(emb_a, 1)

            def high_parts(b, half, w):
                dst, bias = ((q_st, bq_s), (k_hi, bk))[w]
                act.wait_ge(proj_qk, 4 * b + 2 * half + w + 1)
                nc.scalar.activation(dst[:, b, 512 * half:512 * half + 512], bank[proj_banks[b][2 * half + w]],
                                     ACT.Identity, bias=bias[:, 0:1]).then_inc(qk_act, 1)

            def softmax(t):
                act.wait_ge(maxed, t + 1)
                if t >= 2:
                    act.wait_ge(pt_done, t - 1)
                nc.scalar.activation(prob[:, t % 2, :], quad[:, 2 * (t % 2):2 * (t % 2) + 2, :].rearrange("p a n -> p (a n)"),
                                     ACT.Exp, bias=neg_max[:, t:t + 1], accum_out=row_sum[:, t:t + 1]).then_inc(expd, 1)

            def copy_turned(t):
                g = t // 4
                if g >= 2 and t % 4 == 0:
                    act.wait_ge(pv_done, 4 * (g - 1))
                act.wait_ge(pt_done, t + 1)
                nc.scalar.copy(prob_t[:, g % 2, :, P * (t % 4):P * (t % 4) + P],
                               turned.rearrange("p a (k n) -> p (a k) n", n=P)).then_inc(pt_ready, 1)

            def ctx_copy(g):
                act.wait_ge(pv_done, 4 * g + 4)
                if g >= 2:
                    act.wait_ge(ctx_tok, g - 1)
                nc.scalar.copy(ctx_t[:, g % 2, :], PV).then_inc(ctx_ready, 1)

            def xs_copy(g):
                act.wait_ge(hl_t, g + 1)
                nc.scalar.copy(xs[:, g, :], MISC).then_inc(xs_ready, 1)

            def xm_copy(g):
                act.wait_ge(hm_t, g + 1)
                nc.scalar.copy(xm[:, g, :], MISC).then_inc(xm_ready, 1)

            def gelu(u):
                act.wait_ge(pre_done, u + 1)
                if u >= 2:
                    act.wait_ge(down_done, u - 1)
                nc.scalar.activation(hid[:, u % 2, :, :], quad[:, 2 * (u % 2):2 * (u % 2) + 2, :],
                                     ACT.Gelu).then_inc(hid_ready, 1)

            def ffn_copy(g):
                act.wait_ge(down_done, 4 * g + 4)
                if g >= 2:
                    act.wait_ge(y_done, g - 1)
                nc.scalar.copy(ffn_t[:, g % 2, :], DOWN[g % 2]).then_inc(ffn_ready, 1)

            emb(0)
            emb(1)
            emb(2)
            act.wait_ge(scaled, 1)
            for n in range(4):
                high_parts(0, n // 2, n % 2)
            emb(3)
            softmax(0)
            high_parts(1, 0, 0)
            high_parts(1, 0, 1)
            high_parts(1, 1, 0)
            high_parts(1, 1, 1)
            for step in range(STEPS):
                if step < NT:
                    if step + 1 < NT:
                        softmax(step + 1)
                    copy_turned(step)
                else:
                    gelu(step - NT)
                for g in range(G):
                    if step == 4 * g + 7:
                        ctx_copy(g)
                    for at, stage in POST_PE:
                        if step == 4 * g + at and stage in (1, 3):
                            (xs_copy if stage == 1 else xm_copy)(g)
                    if step == FFN_OUT + 4 * g - 1:
                        ffn_copy(g)
            ffn_copy(G - 1)

        @block.vector
        def _(dve):
            chain = [0]

            def link(ins):
                chain[0] += 1
                ins.then_inc(dchain, 1)
                dve.wait_ge(dchain, chain[0])

            dve.wait_ge(wbuild, 1)
            wv = bank[0][:, 0:288].rearrange("p (o i n) -> p i n o", i=OI, n=9)
            for half in range(2):
                dst = tokw[:, :, D * half:D * half + D].rearrange("p r (i o) -> p i r o", i=OI)[:, :, :, 0:8]
                last = nc.vector.tensor_copy(dst, wv[:, :, 4 * half:4 * half + 4, :])
            last = nc.vector.tensor_copy(tokw_pad[:, :].rearrange("p (i o) -> p i o", i=OI)[:, :, 0:8], wv[:, :, 8, :])
            last.then_inc(tokw_ready, 1)

            def emb(k):
                b, c = k // 2, k % 2
                dve.wait_ge(tok_done, k + 1)
                src = bank[TOK_BANK[k]][C:P, :].rearrange("p (j v) -> p j v", v=V)
                if c:
                    nc.vector.tensor_copy(emb2[C:P, b, TILES - 1, :, 0], src[:, 0, :])
                nc.vector.tensor_copy(emb2[C:P, b, 0:TILES - 1, :, c], src[:, 1:TILES, :]).then_inc(emb_b, 1)

            def low_parts(b, half):
                sl = slice(512 * half, 512 * half + 512)
                dve.wait_ge(qk_act, 4 * b + 2 * half + 1)
                nc.vector.scalar_tensor_tensor(q_st[D:P, b, sl], bank[proj_banks[b][2 * half]][D:P, :], bq_s[D:P, 0:1],
                                               q_st[D:P, b, sl].bitcast(F32), op0=ALU.add, op1=ALU.subtract)\
                    .then_inc(qk_dve, 1)
                dve.wait_ge(qk_act, 4 * b + 2 * half + 2)
                nc.vector.scalar_tensor_tensor(k_lo[:, b, sl], bank[proj_banks[b][2 * half + 1]], bk,
                                               k_hi[:, b, sl].bitcast(F32), op0=ALU.add, op1=ALU.subtract)\
                    .then_inc(qk_dve, 1)

            def v_emb(b, half):
                dve.wait_ge(proj_v, 2 * b + half + 1)
                t0 = TILES * b + 4 * half
                nc.vector.tensor_tensor(ve[:, t0:t0 + 4, :], bank[proj_banks[b][4 + half]].rearrange("p (i n) -> p i n", i=4),
                                        bv_0.unsqueeze(1).to_broadcast([P, 4, P]), ALU.add).then_inc(ve_ready, 1)

            def rowmax(t):
                dve.wait_ge(scores, t + 1)
                nc.vector.tensor_reduce(neg_max[:, t:t + 1],
                                        quad[:, 2 * (t % 2):2 * (t % 2) + 2, :].rearrange("p a n -> p (a n)"),
                                        axis=AX_X, op=ALU.max, negate=True).then_inc(maxed, 1)

            def statistics(stats, pairs, sums):
                for i in range(4):
                    last = nc.vector.bn_stats(stats[:, i, :], sums[:, i, :])
                link(last)
                for i in range(4):
                    last = nc.vector.bn_aggr(pairs[:, i, :], stats[:, i, :])
                link(last)

            def inverse_root(work, pairs):
                a, y, z = work[:, :, 0], work[:, :, 1], work[:, :, 2]
                link(nc.vector.tensor_scalar(a, pairs[:, :, 1], EPS, None, ALU.add))
                link(nc.vector.tensor_scalar(y.bitcast(I32), a.bitcast(I32), -0.5, RSQRT_MAGIC, ALU.mult, ALU.add))
                for _ in range(NEWTON):
                    link(nc.vector.scalar_tensor_tensor(z, y, -0.5, y, op0=ALU.mult, op1=ALU.mult))
                    link(nc.vector.tensor_tensor(z, z, a, ALU.mult))
                    link(nc.vector.scalar_tensor_tensor(y, z, 1.5, y, op0=ALU.add, op1=ALU.mult))

            def residual1(g):
                link(nc.vector.reciprocal(row_inv[:, 4 * g:4 * g + 4], row_sum[:, 4 * g:4 * g + 4]))
                dve.wait_ge(ctx_tok, g + 1)
                for i in range(4):
                    t = 4 * g + i
                    last = nc.vector.scalar_tensor_tensor(res1[:, i, :], MISC[:, D * i:D * i + D], row_inv[:, t:t + 1],
                                                          ve[:, t, D:2 * D], op0=ALU.mult, op1=ALU.add)
                last.then_inc(res1_ready, 1)
                dve.wait_ge(res1_ready, g + 1)
                statistics(bst, mv, res1)

            def norm1(g):
                inverse_root(nw, mv)
                for i in range(4):
                    last = nc.vector.tensor_scalar(h1[:, 4 * g + i, :], res1[:, i, :], mv[:, i, 0:1], nw[:, i, 1:2],
                                                   ALU.subtract, ALU.mult)
                last.then_inc(h1_ready, 1)
                dve.wait_ge(h1_ready, g + 1)
                s, hv = g % 2, h1[:, 4 * g:4 * g + 4, :]
                link(nc.vector.tensor_copy(hl[:, s, :, 0:D].bitcast(F32R), hv))
                nc.vector.tensor_tensor(hl[:, s, :, D:P], hv, hl[:, s, :, 0:D], ALU.subtract).then_inc(h_split, 1)

            def choose(g):
                s = g % 2
                dve.wait_ge(gates, g + 1)
                if g == 0:
                    dve.wait_ge(consts, 1)
                if g >= 2:
                    dve.wait_ge(hm_t, g - 1)
                link(nc.vector.tensor_tensor(gate[:, :, :], MISC[:, 0:4 * E].rearrange("p (i e) -> p i e", e=E),
                                             bg.unsqueeze(1).to_broadcast([P, 4, E]), ALU.add))
                link(nc.vector.tensor_tensor(ahead[:, :, :, :], gate[:, :, :].unsqueeze(2).to_broadcast([P, 4, E, E]),
                                             gate[:, :, :].unsqueeze(3).to_broadcast([P, 4, E, E]), ALU.subtract))
                flat = ahead[:, :, :, :].rearrange("p i e j -> p i (e j)")
                link(nc.vector.scalar_tensor_tensor(tied[:, :, :], flat, 0.0, before.unsqueeze(1).to_broadcast([P, 4, E * E]),
                                                    op0=ALU.is_equal, op1=ALU.mult))
                link(nc.vector.scalar_tensor_tensor(beaten[:, :, :], flat, 0.0, tied[:, :, :], op0=ALU.is_gt, op1=ALU.add))
                link(nc.vector.tensor_reduce(rank[:, :, :], beaten[:, :, :].rearrange("p i (e j) -> p i e j", e=E),
                                             axis=AX_X, op=ALU.add))
                for low in (0, R_LOW):
                    nc.vector.tensor_scalar(hm[:, s, :, R_SEL + low:R_SEL + low + E], rank[:, :, :], 1.5, None, ALU.is_lt)
                nc.vector.tensor_scalar(hm[:, s, :, R_OFF:R_OFF + E], rank[:, :, :], 1.5, None, ALU.is_gt).then_inc(mask_ready, 1)

            def norm2(g):
                dve.wait_ge(y_done, g + 1)
                if g >= 1:
                    dve.wait_ge(fin_ready, g)
                nc.vector.tensor_tensor(res2[:, :, :], PV[:, 0:4 * D].rearrange("p (i d) -> p i d", d=D),
                                        h1[:, 4 * g:4 * g + 4, :], ALU.add).then_inc(res2_ready, 1)
                dve.wait_ge(res2_ready, g + 1)
                statistics(bst, mv, res2)
                inverse_root(nw, mv)
                for i in range(4):
                    last = nc.vector.tensor_scalar(fin[:, g, i, :], res2[:, i, :], mv[:, i, 0:1], nw[:, i, 1:2],
                                                   ALU.subtract, ALU.mult)
                last.then_inc(fin_ready, 1)

            dve.wait_ge(ld_attn, 16)
            nc.vector.tensor_scalar(wq_s[:, :], wq2, D ** -0.5, None, ALU.mult)
            nc.vector.tensor_scalar(bq_s[:, :], bq, D ** -0.5, None, ALU.mult).then_inc(scaled, 1)
            dve.wait_ge(scaled, 1)
            emb(0)
            emb(1)
            emb(2)
            low_parts(0, 0)
            low_parts(0, 1)
            v_emb(0, 0)
            emb(3)
            rowmax(0)
            v_emb(0, 1)
            rowmax(1)
            low_parts(1, 0)
            low_parts(1, 1)
            v_emb(1, 0)
            v_emb(1, 1)
            for step in range(STEPS):
                if step + 2 < NT:
                    rowmax(step + 2)
                for g in range(G):
                    if step == 4 * g + 8:
                        residual1(g)
                    if step == 4 * g + 9:
                        norm1(g)
                    if step == 4 * g + 11:
                        choose(g)
                for g in range(G - 1):
                    if step == FFN_OUT + 4 * g:
                        norm2(g)
            norm2(G - 1)

        @block.gpsimd
        def _(pool):
            chain = [0]

            def link(ins):
                chain[0] += 1
                ins.then_inc(pchain, 1)
                pool.wait_ge(pchain, chain[0])

            link(nc.gpsimd.memset(hm[:, :, :, D:P], 0.0))
            hm_lo = hm[:, :, :, D:P].rearrange("p a i (z n) -> p a i z n", n=R_LOW)
            for a in range(2):
                link(nc.gpsimd.memset(hm_lo[:, a, :, :, R_ONE - D], 1.0))
            pool.wait_ge(ld_attn, 16)
            link(nc.gpsimd.tensor_copy(wg_hi[:, :], wg2))
            nc.gpsimd.tensor_tensor(wg_lo[:, :], wg2, wg_hi[:, :].bitcast(F32), ALU.subtract).then_inc(consts, 1)
            pool.wait_ge(consts, 1)
            pool.wait_ge(ld_ffn, 16)
            link(nc.gpsimd.tensor_copy(b2_r[:, :], b2_raw))
            link(nc.gpsimd.tensor_copy(w1_lo[D:P, :, :], w1b_raw[D:P, :, :]))
            link(nc.gpsimd.tensor_copy(w1_hi[:, :, :], w1_raw))
            link(nc.gpsimd.tensor_tensor(b2_r[96:P, :], b2_raw[96:P, :], b2_r[96:P, :].bitcast(F32), ALU.subtract))
            link(nc.gpsimd.tensor_tensor(w1_lo[96:P, :, :], w1b_raw[96:P, :, :], w1_lo[96:P, :, :].bitcast(F32), ALU.subtract))
            nc.gpsimd.tensor_tensor(w1_lo[0:D, :, :], w1b_raw[0:D, :, :], w1_hi[0:D, :, :].bitcast(F32), ALU.subtract)\
                .then_inc(ffnw, 1)
            pool.wait_ge(ffnw, 1)

            for g in range(G):
                pool.wait_ge(h1_ready, g + 1)
                if g >= 2:
                    pool.wait_ge(hm_t, g - 1)
                nc.gpsimd.tensor_copy(hm[:, g % 2, :, 0:D].bitcast(F32R), h1[:, 4 * g:4 * g + 4, :]).then_inc(h_high, 1)


def dft_columns():
    k, p = np.arange(NFREQ)[:, None], np.arange(PATCH)[None, :]
    angle = 2 * np.pi * k * p / PATCH
    coef = np.concatenate([np.cos(angle), -np.sin(angle)], 0) / np.sqrt(PATCH)
    cols = np.zeros((OI, NCOEF, 2, OI, 9))
    for i in range(OI):
        for q in range(2):
            for h in range(2):
                cols[i, :, q, i, 4 * h:4 * h + 4] = coef[:, 8 * h + 4 * q:8 * h + 4 * q + 4]
        cols[i, :, 1, i, 8] = coef[:, 8:16].sum(1)
    return cols.reshape(OI * NCOEF, 2 * OI * 9).astype(np.float32)


def kernel(**inputs):
    import concourse.bacc as bacc
    from concourse.bass_utils import run_bass_kernel_spmd

    a = {n.removeprefix("L0_"): np.ascontiguousarray(v) for n, v in inputs.items()}
    f4 = np.float32
    w = a["tok_W"].reshape(OI, O2, NCOEF, C).transpose(0, 2, 1, 3).reshape(OI * NCOEF, O2 * C)
    tok_pack = np.concatenate([w, dft_columns()], 1)

    eye = np.eye(D, dtype=f4)
    before = np.tile(np.tril(np.ones((E, E), f4), -1).reshape(1, E * E), (P, 1))
    two = lambda m: np.concatenate([m, m], 0)
    rows = lambda m: np.tile(m.reshape(1, -1), (P, 1))
    attn_pack = np.zeros((P, PA_N), f4)
    attn_pack[:, PA_ID:PA_ID + P] = np.eye(P, dtype=f4)
    attn_pack[:, PA_II:PA_II + D] = two(eye)
    for at, m in ((PA_WQ, a["attn_Wq"]), (PA_WK, a["attn_Wk"])):
        attn_pack[:, at:at + P] = np.concatenate([two(m), two(m)], 1)
    attn_pack[:, PA_WV:PA_WV + P] = np.concatenate([two(a["attn_Wv"]), two(eye)], 1)
    attn_pack[:, PA_BV:PA_BV + D] = rows(a["attn_bv"])
    attn_pack[:, PA_BQ] = two(a["attn_bq"])
    attn_pack[:, PA_BK] = two(a["attn_bk"])
    attn_pack[:, PA_WG:PA_WG + E] = two(a["ffn_Wg"])
    attn_pack[:, PA_BG:PA_BG + E] = rows(a["ffn_bg"])
    attn_pack[:, PA_LT:PA_LT + E * E] = before

    ffn_pack = np.zeros((P, PB_N), f4)
    w1 = a["ffn_W1"].transpose(1, 0, 2).reshape(D, E * H)
    ffn_pack[:, PB_W1:PB_W1 + E * H] = two(w1)
    ffn_pack[0:D, PB_W1B:PB_W1B + E * H] = w1
    off = np.zeros((E, E, H), f4)
    off[np.arange(E), np.arange(E), :] = -BIG
    for low in (0, R_LOW):
        ffn_pack[R_OFF + low:R_OFF + low + E, PB_W1B:PB_W1B + E * H] = off.reshape(E, E * H)
        ffn_pack[R_ONE + low, PB_W1B:PB_W1B + E * H] = a["ffn_b1"].reshape(-1)
        ffn_pack[R_SEL + low:R_SEL + low + E, PB_B2:PB_B2 + D] = a["ffn_b2"]
    ffn_pack[:, PB_W2:PB_W2 + E * D] = a["ffn_W2"].transpose(1, 0, 2).reshape(H, E * D)

    nc = bacc.Bacc("TRN2", target_bir_lowering=False, num_devices=1)
    arrays = {"x_dram": a["x"], "tok_pack": tok_pack, "attn_pack": attn_pack, "ffn_pack": ffn_pack}
    args = [nc.dram_tensor(n, v.shape, F32, kind="ExternalInput").ap() for n, v in arrays.items()]
    args.append(nc.dram_tensor("out_dram", (B, S, D), F32, kind="ExternalOutput").ap())
    vit_layer(nc, *args)
    r = run_bass_kernel_spmd(nc, [arrays], core_ids=[0])
    return r.results[0]["out_dram"]
```

```python
from contextlib import ExitStack

import numpy as np

import concourse.bass as bass
from concourse import mybir

F32 = mybir.dt.float32
F32R = mybir.dt.float32r
I32 = mybir.dt.int32
ALU = mybir.AluOpType
ACT = mybir.ActivationFunctionType
AX_X = mybir.AxisListType.X

P = 128
B, C, T, V = 2, 64, 128, 64
PATCH, STRIDE = 16, 8
NPATCH = T // STRIDE
NFREQ = PATCH // 2 + 1
NCOEF = 2 * NFREQ
D = 64
S = V * NPATCH
E, H = 8, 128
OI, O2 = 7, 10
OP = OI * O2
NCOL = OI * 9
TILES = S // P
NT = B * TILES
G = NT // 4
EPS = 1e-5
BIG = float(2.0 ** 60)
RSQRT_MAGIC = float(0x5F1FFFF9)
NEWTON = ((0.703952253, 0.703952253 * 2.38924456), (0.5 * (1 + 3.2e-7), 1.5 * (1 + 3.2e-7)))

PA_ID, PA_II, PA_WQ, PA_WK, PA_WV = 0, 128, 192, 320, 448
PA_BV, PA_BQ, PA_BK = 576, 704, 705
PA_WG, PA_BG, PA_LT, PA_N = 706, 714, 722, 786
PB_W1, PB_W1B, PB_W2, PB_B2, PB_N = 0, 1024, 2048, 2560, 2688
R_OFF, R_ONE, R_SEL, R_LOW = 64, 72, 73, 32

TOK_BANK = (2, 3, 0, 1)
PAD_BANK = (7, 6)
STEPS = 2 * NT
ON_TENSOR = (
    (8, 2, "ctx", 0), (11, 1, "x", 0), (12, 2, "ctx", 1), (13, 2, "gates", 0), (15, 0, "flags", 0),
    (15, 1, "x", 1), (16, 1, "gates", 1), (17, 1, "ctx", 2), (18, 1, "flags", 1), (19, 1, "x", 2),
    (19, 2, "gates", 2), (21, 1, "ctx", 3), (22, 0, "out", 0), (22, 0, "flags", 2), (24, 0, "x", 3),
    (25, 0, "gates", 3), (25, 1, "out", 1), (26, 1, "flags", 3), (29, 0, "out", 2),
)
ON_SCALAR = (
    (8, 0, "ctx", 0), (11, 1, "ctx", 1), (11, 1, "x", 0), (15, 1, "flags", 0), (15, 1, "ctx", 2),
    (16, 0, "x", 1), (19, 0, "flags", 1), (20, 0, "x", 2), (21, 1, "ctx", 3), (22, 0, "out", 0),
    (23, 0, "flags", 2), (24, 1, "x", 3), (24, 1, "out", 1), (26, 1, "flags", 3), (28, 1, "out", 2),
)
WEIGH = (
    (4, 0, 0), (5, 0, 1), (6, 0, 2), (7, 0, 3), (9, 1, 0), (9, 1, 1), (10, 1, 2), (11, 1, 3), (13, 2, 0),
    (14, 2, 1), (14, 2, 2), (15, 2, 3), (16, 3, 0), (17, 3, 1), (19, 3, 2), (19, 3, 3),
)
ON_VECTOR = (
    (8, 1, "ctx", 0), (10, 0, "stats", 0), (10, 1, "norm", 0), (10, 1, "split", 0), (13, 0, "ctx", 1),
    (14, 0, "stats", 1), (14, 0, "gates", 0), (14, 1, "norm", 1), (14, 1, "split", 1), (15, 1, "gates", 1),
    (16, 1, "ctx", 2), (16, 1, "stats", 2), (17, 1, "norm", 2), (17, 1, "split", 2), (20, 1, "gates", 2),
    (21, 1, "ctx", 3), (22, 0, "stats", 3), (22, 1, "norm", 3), (22, 1, "split", 3), (23, 1, "out", 0),
    (25, 1, "gates", 3), (26, 1, "out", 1), (29, 1, "out", 2),
)
V_STEPS = (1, 3)
POOL_X = (2, 2)
POOL_ROOTS = 2


def vit_layer(nc, x, tok_pack, attn_pack, ffn_pack, out):
    with ExitStack() as ctx:
        def sb(name, shape, dt=F32):
            return ctx.enter_context(nc.sbuf_tensor(name, shape, dt))

        def sem(name):
            return ctx.enter_context(nc.semaphore(name))

        x_sb = sb("x_sb", [P, B, NPATCH, 4, V])
        tok_sb = sb("tok_sb", [OI * NCOEF, O2 * C + 2 * NCOL])
        attn_sb = sb("attn_sb", [P, PA_N])
        ffn_sb = sb("ffn_sb", [P, PB_N])
        x_hi = sb("x_hi", [P, B, NPATCH, 4, V], F32R)
        x_lo = sb("x_lo", [P, B, NPATCH, 4, V], F32R)
        tokw_hi = sb("tokw_hi", [P, 4, D + OP], F32R)
        tokw_lo = sb("tokw_lo", [P, 4, D + OP], F32R)
        padw_hi = sb("padw_hi", [P, D + OP], F32R)
        padw_lo = sb("padw_lo", [P, D + OP], F32R)
        emb_hi = sb("emb_hi", [P, B, TILES, V, 2], F32R)
        emb_lo = sb("emb_lo", [P, B, TILES, V, 2], F32R)
        projw_hi = sb("projw_hi", [P, 3, P], F32R)
        projw_lo = sb("projw_lo", [P, 3, P], F32R)
        idle = sb("idle", [P, 512], mybir.dt.bfloat16)
        ve = sb("ve", [P, NT, 2 * D])
        prob = sb("prob", [P, 2, S])
        neg_max = sb("neg_max", [P, NT])
        row_sum = sb("row_sum", [P, NT])
        row_inv = sb("row_inv", [P, NT])
        ctx_t = sb("ctx_t", [P, 2, 512])
        res1 = sb("res1", [P, 4, D])
        h1 = sb("h1", [P, NT, D])
        res2 = sb("res2", [P, 4, D])
        fin = sb("fin", [P, G, 4, D])
        bst = sb("bst", [P, 4, 6])
        mv = sb("mv", [P, 4, 2])
        bst2 = sb("bst2", [P, 4, 6])
        mv2 = sb("mv2", [P, 4, 2])
        nw2 = sb("nw2", [P, 4, 4])
        nw = sb("nw", [P, 4, 4])
        hl = sb("hl", [P, 2, 4, P])
        hm = sb("hm", [P, 2, 4, P])
        gate = sb("gate", [P, 4, E])
        ahead = sb("ahead", [P, 4, E, E])
        tied = sb("tied", [P, 4, E * E])
        beaten = sb("beaten", [P, 4, E * E])
        rank = sb("rank", [P, 4, E])
        w1_hi = sb("w1_hi", [P, E, H], F32R)
        w1_lo = sb("w1_lo", [P, E, H], F32R)
        wg_r = sb("wg_r", [P, 2 * E], F32R)
        b2_r = sb("b2_r", [P, P], F32R)
        hid = sb("hid", [P, 2, 2, 512])
        ffn_t = sb("ffn_t", [P, 2, 512])

        ps = ctx.enter_context(nc.psum_tensor("ps", [P, 8, 512], F32))
        bank = [ps[:, i, :] for i in range(8)]
        quad = ps[:, 0:4, :]
        turned = ps[:, 4:6, :]
        proj_banks = ((4, 5, 2, 3, 7, 4), (6, 7, 6, 7, 6, 7))
        PV, MISC = bank[6], bank[7]
        DOWN = (bank[4], bank[5])

        ld_tok = sem("ld_tok")
        ld_x = [sem(f"ld_x{i}") for i in range(4)]
        ld_attn = sem("ld_attn")
        ld_ffn = sem("ld_ffn")
        st_out = sem("st_out")
        wbuild = sem("wbuild")
        tokw_ready = sem("tokw_ready")
        tok_done = sem("tok_done")
        pad_done = sem("pad_done")
        idle_ready = sem("idle_ready")
        padw_zero = sem("padw_zero")
        wb_hi = sem("wb_hi")
        xhi_ready = sem("xhi_ready")
        xlo_ready = sem("xlo_ready")
        ehi_ready = sem("ehi_ready")
        elo_ready = sem("elo_ready")
        proj_qk = sem("proj_qk")
        proj_v = sem("proj_v")
        scaled = sem("scaled")
        xlo_pool = sem("xlo_pool")
        wg_ready = sem("wg_ready")
        projw_ready = sem("projw_ready")
        y_read = sem("y_read")
        qk_act = sem("qk_act")
        qk_dve = sem("qk_dve")
        ve_ready = sem("ve_ready")
        scores = sem("scores")
        maxed = sem("maxed")
        expd = sem("expd")
        pt_done = sem("pt_done")
        pt_ready = sem("pt_ready")
        pv_done = sem("pv_done")
        ctx_ready = sem("ctx_ready")
        ctx_tok = sem("ctx_tok")
        res1_ready = sem("res1_ready")
        mv_ready = sem("mv_ready")
        root_ready = sem("root_ready")
        h_high = sem("h_high")
        h1_ready = sem("h1_ready")
        h_split = sem("h_split")
        hl_t = sem("hl_t")
        xs_ready = sem("xs_ready")
        gates = sem("gates")
        mask_ready = sem("mask_ready")
        hm_t = sem("hm_t")
        xm_ready = sem("xm_ready")
        ffnw = sem("ffnw")
        consts = sem("consts")
        pre_done = sem("pre_done")
        hid_ready = sem("hid_ready")
        down_done = sem("down_done")
        ffn_ready = sem("ffn_ready")
        y_done = sem("y_done")
        fin_ready = sem("fin_ready")
        dchain = sem("dchain")
        pchain = sem("pchain")

        tok_w = tok_sb[:, 0:O2 * C].rearrange("p (o c) -> p o c", c=C)
        dft = tok_sb[:, O2 * C:O2 * C + 2 * NCOL].rearrange("p (q n) -> p q n", q=2)
        ident = attn_sb[:, PA_ID:PA_ID + P]
        twin = attn_sb[:, PA_II:PA_II + D]
        twin_r = projw_hi[:, 2, D:P]
        wq2 = attn_sb[:, PA_WQ:PA_WQ + P]
        wk2 = attn_sb[:, PA_WK:PA_WK + P]
        wv_i = attn_sb[:, PA_WV:PA_WV + P]
        bv_0 = attn_sb[:, PA_BV:PA_BV + P]
        bq = attn_sb[:, PA_BQ:PA_BQ + 1]
        bk = attn_sb[:, PA_BK:PA_BK + 1]
        wg2 = attn_sb[:, PA_WG:PA_WG + E]
        bg = attn_sb[:, PA_BG:PA_BG + E]
        before = attn_sb[:, PA_LT:PA_LT + E * E]
        w1_raw = ffn_sb[:, PB_W1:PB_W1 + E * H].rearrange("p (e h) -> p e h", e=E)
        w1b_raw = ffn_sb[:, PB_W1B:PB_W1B + E * H].rearrange("p (e h) -> p e h", e=E)
        w2 = ffn_sb[:, PB_W2:PB_W2 + E * D].rearrange("p (e d) -> p e d", e=E)
        b2_raw = ffn_sb[:, PB_B2:PB_B2 + P]

        wq_s = sb("wq_s", [P, P])
        bq_s = sb("bq_s", [P, 1])

        prob_t = x_sb[:, :, :, :, :].rearrange("p b (k z) r v -> p b k (z r v)", k=TILES)
        x_parts = [t[:, :, :, :, :].rearrange("p b (k m) r v -> p b k (m r v)", k=2) for t in (x_hi, x_lo)]
        q_st, k_hi, k_lo = (a.rearrange("p (b s) -> p b s", b=B)
                            for a in (x_parts[0][:, 0, 0, :], x_parts[1][:, 0, 0, :], x_parts[1][:, 0, 1, :]))
        xs, xm = (x_parts[0][:, 1, k, :].rearrange("p (g n) -> p g n", g=G) for k in range(2))
        e_hi = emb_hi[:, :, :, :, :].rearrange("p b j v n -> p b (j v n)")
        e_lo = emb_lo[:, :, :, :, :].rearrange("p b j v n -> p b (j v n)")

        def built(hb):
            return bank[hb][:, 0:O2 // 2 * NCOL].rearrange("p (o i n) -> p i n o", i=OI, n=9)

        def places(main, pad, hb):
            src, n = built(hb), O2 // 2
            o2 = slice(n * hb, n * hb + n)
            by_o = lambda w, pat: w.rearrange(pat, i=OI)
            parts = [(by_o(main[:, :, D:D + OP], "p r (o i) -> p i r o")[:, :, :, o2], src[:, :, 4:8, :]),
                     (by_o(pad[:, D:D + OP], "p (o i) -> p i o")[:, :, o2], src[:, :, 8, :])]
            first = by_o(main[:, :, 0:OP], "p r (o i) -> p i r o")
            if hb == 0:
                return [(first[:, :, :, o2], src[:, :, 0:4, :])] + parts
            return [(first[:, :, :, n:O2 - 1], src[:, :, 0:4, 0:n - 1]), (main[:, :, D - 1], src[:, 0, 0:4, n - 1])] + parts

        def down_pieces(g):
            if g < G - 1:
                return ((slice(0, 512), DOWN[g % 2]),)
            return (slice(0, 256), DOWN[g % 2][:, 0:256]), (slice(256, 512), MISC[:, 0:256])

        def y_parts(g):
            return (((0, 1, 2, 3), PV),) if g < G - 1 else (((0, 1), PV), ((2, 3), DOWN[0]))

        def chunk_parts(k):
            b, c = k // 2, k % 2
            src = bank[TOK_BANK[k]].rearrange("p (j v) -> p j v", v=V)
            part_a = [((slice(0, C), b, slice(0, TILES), slice(0, V), c), src[0:C, :, :])]
            part_b = [((slice(C, P), b, slice(0, TILES - 1), slice(0, V), c), src[C:P, 1:TILES, :])]
            if c:
                part_b += [((slice(C, P), b, TILES - 1, slice(0, V), 0), src[C:P, 0, :]),
                           ((slice(C, P), b, TILES - 1, slice(0, V), 1), bank[PAD_BANK[b]][C:P, 0:V])]
            return part_a, part_b

        block = ctx.enter_context(nc.Block())

        @block.sync
        def _(sp):
            sp.dma_start(tok_sb[:, :], tok_pack).then_inc(ld_tok, 16)
            xv = x.rearrange("b c (m q r) v -> b q c m (r v)", q=2, r=4)
            for k in range(4):
                b, m = k // 2, 8 * (k % 2)
                for q in range(2):
                    sp.dma_start(x_sb[q * C:(q + 1) * C, b, m:m + 8, :, :].rearrange("c m r v -> c m (r v)"),
                                 xv[b, q, :, m:m + 8, :]).then_inc(ld_x[k], 16)
            sp.dma_start(attn_sb[:, :], attn_pack).then_inc(ld_attn, 16)
            sp.dma_start(ffn_sb[:, :], ffn_pack).then_inc(ld_ffn, 16)
            ov = out.rearrange("b (p j) d -> b p j d", j=TILES)
            for g in range(G):
                sp.wait_ge(fin_ready, g + 1)
                sp.dma_start(ov[g // 2, :, 4 * (g % 2):4 * (g % 2) + 4, :], fin[:, g, :, :]).then_inc(st_out, 16)
            sp.wait_ge(st_out, 16 * G)

        @block.tensor
        def _(pe):
            def keep_warm(n):
                for _ in range(n):
                    nc.tensor.matmul(MISC, idle[:, 0:P], idle[:, :], start=True, stop=True)

            pe.wait_ge(idle_ready, 1)
            keep_warm(8)
            pe.wait_ge(ld_tok, 16)
            for hb in range(2):
                for i in range(O2 // 2):
                    for q in range(2):
                        last = nc.tensor.matmul(bank[hb][q * C:(q + 1) * C, NCOL * i:NCOL * i + NCOL],
                                                tok_w[:, O2 // 2 * hb + i, :], dft[:, q, :], start=True, stop=True)
                last.then_inc(wbuild, 1)
            keep_warm(4)

            def products(dst, pairs):
                for n, (w, v) in enumerate(pairs):
                    last = nc.tensor.matmul(dst, w, v, start=(n == 0), stop=(n == len(pairs) - 1))
                return last

            def tokens(k):
                b, m = k // 2, 8 * (k % 2)
                hi, lo = ([t[:, b, m:m + 8, r, :] for r in range(4)] for t in (x_hi, x_lo))
                dst = bank[TOK_BANK[k]]
                if k == 0:
                    pe.wait_ge(wb_hi, 2)
                for r in range(4):
                    if r % 2 == 0:
                        pe.wait_ge(xhi_ready, 2 * k + r // 2 + 1)
                    nc.tensor.matmul(dst, tokw_hi[:, r, 0:P], hi[r], start=(r == 0), stop=False)
                if k == 0:
                    pe.wait_ge(tokw_ready, 2)
                for r in range(4):
                    nc.tensor.matmul(dst, tokw_lo[:, r, 0:P], hi[r], start=False, stop=False)
                for r in range(4):
                    if (k, r) == POOL_X:
                        pe.wait_ge(xlo_pool, 1)
                    elif r % 2 == 0:
                        pe.wait_ge(xlo_ready, 2 * k + r // 2 + 1 - ((k, r) > POOL_X))
                    last = nc.tensor.matmul(dst, tokw_hi[:, r, 0:P], lo[r], start=False, stop=(r == 3))
                last.then_inc(tok_done, 1)
                if k % 2:
                    pe.wait_ge(padw_zero, 1)
                    hi, lo = x_hi[:, b, NPATCH - 1, 3, :], x_lo[:, b, NPATCH - 1, 3, :]
                    products(bank[PAD_BANK[b]][:, 0:V],
                             [(padw_hi[:, 0:P], hi), (padw_lo[:, 0:P], hi), (padw_hi[:, 0:P], lo)]).then_inc(pad_done, 1)

            def project_qk(b, half, w):
                sl = slice(512 * half, 512 * half + 512)
                hi, lo = e_hi[:, b, sl], e_lo[:, b, sl]
                products(bank[proj_banks[b][2 * half + w]],
                         [(projw_hi[:, w, :], hi), (projw_lo[:, w, :], hi), (projw_hi[:, w, :], lo)]).then_inc(proj_qk, 1)

            def project_v(b, half):
                for i in range(4):
                    sl = slice(P * (4 * half + i), P * (4 * half + i) + P)
                    hi, lo = e_hi[:, b, sl], e_lo[:, b, sl]
                    last = products(bank[proj_banks[b][4 + half]][:, P * i:P * i + P],
                                    [(hi, projw_hi[:, 2, :]), (hi, projw_lo[:, 2, :]), (lo, projw_hi[:, 2, :])])
                last.then_inc(proj_v, 1)

            def score(t):
                b, j = t // TILES, t % TILES
                for half in range(2):
                    ks = slice(512 * half, 512 * half + 512)
                    dst = quad[:, 2 * (t % 2) + half, :]
                    nc.tensor.matmul(dst, q_st[:, b, P * j:P * j + P], k_hi[:, b, ks], start=True, stop=False)
                    last = nc.tensor.matmul(dst, q_st[:, b, P * j:P * j + P], k_lo[:, b, ks], start=False, stop=True)
                last.then_inc(scores, 1)

            def turn(t):
                pe.wait_ge(expd, t + 1)
                if t >= 1:
                    pe.wait_ge(pt_ready, t)
                for kb in range(TILES):
                    last = nc.tensor.transpose(turned[:, kb // 4, P * (kb % 4):P * (kb % 4) + P],
                                               prob[:, t % 2, P * kb:P * kb + P], ident)
                last.then_inc(pt_done, 1)

            def weigh(g, i):
                if i == 0:
                    pe.wait_ge(pt_ready, 4 * g + 4)
                    pe.wait_ge(*((ctx_ready, g) if g else (ve_ready, 3)))
                for half in range(2):
                    kb = 2 * i + half
                    last = nc.tensor.matmul(PV[half * D:(half + 1) * D, :], ve[:, (g // 2) * TILES + kb, 0:D],
                                            prob_t[:, g % 2, kb, :], start=(i == 0), stop=(i == 3))
                last.then_inc(pv_done, 1)

            misc_read = [(ve_ready, 4)]

            def misc_free():
                pe.wait_ge(*misc_read[0])

            def group_work(step, place):
                for at, where, what, g in ON_TENSOR:
                    if (at, where) != (step, place):
                        continue
                    if what == "out":
                        ffn_to_tokens(g)
                        continue
                    do, reader = {"ctx": (ctx_to_tokens, res1_ready), "x": (turn_x, xs_ready),
                                  "gates": (gate_scores, mask_ready), "flags": (turn_flags, xm_ready)}[what]
                    do(g)
                    misc_read[0] = (reader, g + 1)

            def ctx_to_tokens(g):
                pe.wait_ge(ctx_ready, g + 1)
                misc_free()
                for i in range(4):
                    last = nc.tensor.matmul(MISC[:, D * i:D * i + D], ctx_t[:, g % 2, P * i:P * i + P], twin,
                                            start=True, stop=True)
                last.then_inc(ctx_tok, 1)

            def turn_x(g):
                pe.wait_ge(h_split, g + 1)
                misc_free()
                for i in range(4):
                    last = nc.tensor.transpose(MISC[:, P * i:P * i + P], hl[:, g % 2, i, :], ident)
                last.then_inc(hl_t, 1)

            def gate_scores(g):
                pe.wait_ge(xs_ready, g + 1)
                if g == 0:
                    pe.wait_ge(wg_ready, 1)
                misc_free()
                for i in range(4):
                    last = nc.tensor.matmul(MISC[:, 2 * E * i:2 * E * i + 2 * E], xs[:, g, P * i:P * i + P], wg_r[:, :],
                                            start=True, stop=True)
                last.then_inc(gates, 1)

            def turn_flags(g):
                pe.wait_ge(mask_ready, g + 1)
                pe.wait_ge(h_high, g + 1)
                misc_free()
                for i in range(4):
                    last = nc.tensor.transpose(MISC[:, P * i:P * i + P], hm[:, g % 2, i, :], ident)
                last.then_inc(hm_t, 1)

            def up(u):
                g, i = u // 4, u % 4
                if i == 0:
                    pe.wait_ge(xm_ready, g + 1)
                if u >= 2:
                    pe.wait_ge(hid_ready, u - 1)
                for half in range(2):
                    e = 2 * i + half
                    dst = quad[:, 2 * (u % 2) + half, :]
                    nc.tensor.matmul(dst, w1_hi[:, e, :], xs[:, g, :], start=True, stop=False)
                    last = nc.tensor.matmul(dst, w1_lo[:, e, :], xm[:, g, :], start=False, stop=True)
                last.then_inc(pre_done, 1)

            def down(u):
                g, i = u // 4, u % 4
                pe.wait_ge(hid_ready, u + 1)
                if i == 0 and g >= 2:
                    pe.wait_ge(ffn_ready, g - 1)
                for n, (cols, dst) in enumerate(down_pieces(g)):
                    if i == 0:
                        nc.tensor.matmul(dst, b2_r[:, :], xm[:, g, cols], start=True, stop=False)
                        nc.tensor.matmul(dst[0:D, :], twin_r, xs[:, g, cols], start=False, stop=False)
                    if u == NT - 1 and n == 1:
                        pe.wait_ge(hid_ready, NT + 1)
                    for half in range(2):
                        last = nc.tensor.matmul(dst[half * D:(half + 1) * D, :], w2[:, 2 * i + half, :],
                                                hid[:, u % 2, half, cols], start=False, stop=(i == 3))
                    if u == NT - 1 and n == 0:
                        last.then_inc(down_done, 1)
                last.then_inc(down_done, 1)

            def ffn_to_tokens(g):
                if g >= 1:
                    pe.wait_ge(y_read, g)
                for n, (tiles, dst) in enumerate(y_parts(g)):
                    pe.wait_ge(ffn_ready, g + 1 + n)
                    for k, i in enumerate(tiles):
                        src = ffn_t[:, g % 2, P * i:P * i + P]
                        if g < G - 1:
                            last = nc.tensor.transpose(dst[:, P * k:P * k + P], src, ident)
                        else:
                            last = nc.tensor.matmul(dst[:, D * k:D * k + D], src, twin, start=True, stop=True)
                    last.then_inc(y_done, 1)

            tokens(0)
            tokens(1)
            tokens(2)
            tokens(3)
            pe.wait_ge(elo_ready, 4)
            for n in range(4):
                if n < 2:
                    pe.wait_ge(projw_ready, n + 1)
                project_qk(0, n // 2, n % 2)
            pe.wait_ge(projw_ready, 3)
            project_v(0, 0)
            pe.wait_ge(qk_dve, 1)
            project_v(0, 1)
            pe.wait_ge(qk_dve, 4)
            pe.wait_ge(elo_ready, 6)
            pe.wait_ge(elo_ready, 8)
            score(0)
            score(1)
            pe.wait_ge(ve_ready, 1)
            project_qk(1, 0, 0)
            project_qk(1, 0, 1)
            for step in range(STEPS):
                if step < NT:
                    if step == 0:
                        pe.wait_ge(ve_ready, 2)
                    turn(step)
                    group_work(step, 0)
                    if step + 2 < NT:
                        score(step + 2)
                    if step == 0:
                        for w in range(2):
                            pe.wait_ge(qk_dve, 5 + w)
                            project_qk(1, 1, w)
                    if step in V_STEPS:
                        half = V_STEPS.index(step)
                        pe.wait_ge(qk_dve, 7 + half)
                        project_v(1, half)
                else:
                    u = step - NT
                    group_work(step, 0)
                    if u == 0:
                        pe.wait_ge(ffnw, 1)
                        up(0)
                    if u + 1 < NT:
                        up(u + 1)
                for at, g, i in WEIGH:
                    if at == step:
                        weigh(g, i)
                group_work(step, 1)
                if step >= NT:
                    down(step - NT)
                group_work(step, 2)
            ffn_to_tokens(G - 1)

        @block.scalar
        def _(act):
            def tok_weights(hb):
                act.wait_ge(wbuild, hb + 1)
                for dst, src in places(tokw_hi, padw_hi, hb):
                    last = nc.scalar.copy(dst, src)
                last.then_inc(wb_hi, 1)

            def x_high(k, parts=(0, 2)):
                b, m = k // 2, 8 * (k % 2)
                act.wait_ge(ld_x[k], 32)
                for rr in parts:
                    nc.scalar.copy(x_hi[:, b, m:m + 8, rr:rr + 2, :], x_sb[:, b, m:m + 8, rr:rr + 2, :]).then_inc(xhi_ready, 1)

            def emb(k):
                act.wait_ge(tok_done, k + 1)
                if k % 2:
                    act.wait_ge(pad_done, k // 2 + 1)
                for part in chunk_parts(k):
                    for dst, src in part:
                        ins = nc.scalar.copy(emb_hi[dst], src)
                    ins.then_inc(ehi_ready, 1)

            def high_parts(b, half, w):
                dst, bias = ((q_st, bq_s), (k_hi, bk))[w]
                act.wait_ge(proj_qk, 4 * b + 2 * half + w + 1)
                nc.scalar.activation(dst[:, b, 512 * half:512 * half + 512], bank[proj_banks[b][2 * half + w]],
                                     ACT.Identity, bias=bias[:, 0:1]).then_inc(qk_act, 1)

            def softmax(t):
                act.wait_ge(maxed, t + 1)
                if t >= 2:
                    act.wait_ge(pt_done, t - 1)
                nc.scalar.activation(prob[:, t % 2, :], quad[:, 2 * (t % 2):2 * (t % 2) + 2, :].rearrange("p a n -> p (a n)"),
                                     ACT.Exp, bias=neg_max[:, t:t + 1], accum_out=row_sum[:, t:t + 1]).then_inc(expd, 1)

            def copy_turned(t):
                g = t // 4
                if g >= 2 and t % 4 == 0:
                    act.wait_ge(pv_done, 4 * (g - 1))
                act.wait_ge(pt_done, t + 1)
                nc.scalar.copy(prob_t[:, g % 2, :, P * (t % 4):P * (t % 4) + P],
                               turned.rearrange("p a (k n) -> p (a k) n", n=P)).then_inc(pt_ready, 1)

            def ctx_copy(g):
                act.wait_ge(pv_done, 4 * g + 4)
                if g >= 2:
                    act.wait_ge(ctx_tok, g - 1)
                nc.scalar.copy(ctx_t[:, g % 2, :], PV).then_inc(ctx_ready, 1)

            def xs_copy(g):
                act.wait_ge(hl_t, g + 1)
                nc.scalar.copy(xs[:, g, :], MISC).then_inc(xs_ready, 1)

            def xm_copy(g):
                act.wait_ge(hm_t, g + 1)
                nc.scalar.copy(xm[:, g, :], MISC).then_inc(xm_ready, 1)

            def gelu(u):
                act.wait_ge(pre_done, u + 1)
                if u >= 2:
                    act.wait_ge(down_done, u - 1)
                for cols in (slice(0, 256), slice(256, 512)) if u == NT - 1 else (slice(0, 512),):
                    nc.scalar.activation(hid[:, u % 2, :, cols], quad[:, 2 * (u % 2):2 * (u % 2) + 2, cols],
                                         ACT.Gelu).then_inc(hid_ready, 1)

            def ffn_copy(g):
                if g >= 2:
                    act.wait_ge(y_done, g - 1)
                for n, (cols, src) in enumerate(down_pieces(g)):
                    act.wait_ge(down_done, 4 * g + 4 + n)
                    nc.scalar.copy(ffn_t[:, g % 2, cols], src).then_inc(ffn_ready, 1)

            def group_work(step, place):
                for at, where, what, g in ON_SCALAR:
                    if (at, where) == (step, place):
                        {"ctx": ctx_copy, "x": xs_copy, "flags": xm_copy, "out": ffn_copy}[what](g)

            tok_weights(0)
            x_high(0, (0,))
            tok_weights(1)
            x_high(0, (2,))
            x_high(1)
            x_high(2)
            emb(0)
            x_high(3)
            emb(1)
            emb(2)
            act.wait_ge(scaled, 1)
            emb(3)
            for n in range(4):
                high_parts(0, n // 2, n % 2)
            softmax(0)
            high_parts(1, 0, 0)
            high_parts(1, 0, 1)
            for step in range(STEPS):
                group_work(step, 0)
                if step < NT:
                    if step + 1 < NT:
                        softmax(step + 1)
                    copy_turned(step)
                    if step == 0:
                        high_parts(1, 1, 0)
                        high_parts(1, 1, 1)
                else:
                    gelu(step - NT)
                group_work(step, 1)
            ffn_copy(G - 1)

        @block.vector
        def _(dve):
            chain = [0]

            def link(ins, meanwhile=None):
                chain[0] += 1
                ins.then_inc(dchain, 1)
                if meanwhile:
                    meanwhile()
                dve.wait_ge(dchain, chain[0])

            def tok_weights(hb):
                dve.wait_ge(wb_hi, hb + 1)
                for (dst, src), (hi, _) in zip(places(tokw_lo, padw_lo, hb), places(tokw_hi, padw_hi, hb)):
                    last = nc.vector.tensor_tensor(dst, src, hi.bitcast(F32), ALU.subtract)
                last.then_inc(tokw_ready, 1)

            def x_low(k, parts=(0, 2)):
                b, m = k // 2, 8 * (k % 2)
                for rr in parts:
                    dve.wait_ge(xhi_ready, 2 * k + rr // 2 + 1)
                    nc.vector.tensor_tensor(x_lo[:, b, m:m + 8, rr:rr + 2, :], x_sb[:, b, m:m + 8, rr:rr + 2, :],
                                            x_hi[:, b, m:m + 8, rr:rr + 2, :].bitcast(F32), ALU.subtract).then_inc(xlo_ready, 1)

            def emb(k):
                for n, part in enumerate(chunk_parts(k)):
                    dve.wait_ge(ehi_ready, 2 * k + n + 1)
                    for dst, src in part:
                        ins = nc.vector.tensor_tensor(emb_lo[dst], src, emb_hi[dst].bitcast(F32), ALU.subtract)
                    ins.then_inc(elo_ready, 1)

            def low_parts(b, half):
                sl = slice(512 * half, 512 * half + 512)
                dve.wait_ge(qk_act, 4 * b + 2 * half + 1)
                nc.vector.scalar_tensor_tensor(q_st[D:P, b, sl], bank[proj_banks[b][2 * half]][D:P, :], bq_s[D:P, 0:1],
                                               q_st[D:P, b, sl].bitcast(F32), op0=ALU.add, op1=ALU.subtract)\
                    .then_inc(qk_dve, 1)
                dve.wait_ge(qk_act, 4 * b + 2 * half + 2)
                nc.vector.scalar_tensor_tensor(k_lo[:, b, sl], bank[proj_banks[b][2 * half + 1]], bk,
                                               k_hi[:, b, sl].bitcast(F32), op0=ALU.add, op1=ALU.subtract)\
                    .then_inc(qk_dve, 1)

            def v_emb(b, half):
                dve.wait_ge(proj_v, 2 * b + half + 1)
                t0 = TILES * b + 4 * half
                nc.vector.tensor_tensor(ve[:, t0:t0 + 4, :], bank[proj_banks[b][4 + half]].rearrange("p (i n) -> p i n", i=4),
                                        bv_0.unsqueeze(1).to_broadcast([P, 4, P]), ALU.add).then_inc(ve_ready, 1)

            def rowmax(t):
                dve.wait_ge(scores, t + 1)
                nc.vector.tensor_reduce(neg_max[:, t:t + 1],
                                        quad[:, 2 * (t % 2):2 * (t % 2) + 2, :].rearrange("p a n -> p (a n)"),
                                        axis=AX_X, op=ALU.max, negate=True).then_inc(maxed, 1)

            def aggregate(pairs, stats, signal=None):
                for i in range(4):
                    last = nc.vector.bn_aggr(pairs[:, i, :], stats[:, i, :])
                if signal:
                    last.then_inc(signal, 1)
                else:
                    link(last)

            def statistics(stats, pairs, sums, signal=None):
                for i in range(4):
                    last = nc.vector.bn_stats(stats[:, i, :], sums[:, i, :])
                link(last)
                aggregate(pairs, stats, signal)

            def add_halves(dst, src):
                return nc.vector.tensor_reduce(dst[:, :, :], src.rearrange("p (i h n) -> p i n h", h=2, i=4),
                                               axis=AX_X, op=ALU.add)

            def centre(dst, sums, pairs, at=0):
                mean = pairs[:, at:at + 2, 0].unsqueeze(2).to_broadcast([P, 2, D])
                return nc.vector.tensor_tensor(dst[:, at:at + 2, :], sums, mean, ALU.subtract)

            def centre_and_root(dst, sums, work, pairs):
                a, y, z = work[:, :, 0], work[:, :, 1], work[:, :, 2]
                link(nc.vector.tensor_scalar(a, pairs[:, :, 1], EPS, None, ALU.add),
                     lambda: centre(dst, sums[0], pairs))
                link(nc.vector.tensor_scalar(y.bitcast(I32), a.bitcast(I32), -0.5, RSQRT_MAGIC, ALU.mult, ALU.add),
                     lambda: centre(dst, sums[1], pairs, 2))
                for c3, c1 in NEWTON:
                    link(nc.vector.scalar_tensor_tensor(z, y, -c3, y, op0=ALU.mult, op1=ALU.mult))
                    link(nc.vector.tensor_tensor(z, z, a, ALU.mult))
                    link(nc.vector.scalar_tensor_tensor(y, z, c1, y, op0=ALU.add, op1=ALU.mult))

            def residual1(g):
                link(nc.vector.reciprocal(row_inv[:, 4 * g:4 * g + 4], row_sum[:, 4 * g:4 * g + 4]))
                dve.wait_ge(ctx_tok, g + 1)
                for i in range(4):
                    t = 4 * g + i
                    last = nc.vector.scalar_tensor_tensor(res1[:, i, :], MISC[:, D * i:D * i + D], row_inv[:, t:t + 1],
                                                          ve[:, t, D:2 * D], op0=ALU.mult, op1=ALU.add)
                last.then_inc(res1_ready, 1)

            def statistics1(g):
                dve.wait_ge(res1_ready, g + 1)
                statistics(bst, mv, res1, mv_ready)
                if g < POOL_ROOTS:
                    dve.wait_ge(mv_ready, g + 1)
                    centre(res1, res1[:, 0:2, :], mv)
                    link(centre(res1, res1[:, 2:4, :], mv, 2))

            def norm1(g):
                if g < POOL_ROOTS:
                    dve.wait_ge(root_ready, g + 1)
                else:
                    dve.wait_ge(mv_ready, g + 1)
                    centre_and_root(res1, (res1[:, 0:2, :], res1[:, 2:4, :]), nw, mv)
                last = nc.vector.tensor_tensor(h1[:, 4 * g:4 * g + 4, :], res1[:, :, :],
                                               nw[:, :, 1].unsqueeze(2).to_broadcast([P, 4, D]), ALU.mult)
                last.then_inc(h1_ready, 1)

            def split_h1(g):
                dve.wait_ge(h1_ready, g + 1)
                s, hv = g % 2, h1[:, 4 * g:4 * g + 4, :]
                link(nc.vector.tensor_copy(hl[:, s, :, 0:D].bitcast(F32R), hv))
                nc.vector.tensor_tensor(hl[:, s, :, D:P], hv, hl[:, s, :, 0:D], ALU.subtract).then_inc(h_split, 1)

            def choose(g):
                s = g % 2
                dve.wait_ge(gates, g + 1)
                if g == 0:
                    dve.wait_ge(consts, 2)
                if g >= 2:
                    dve.wait_ge(hm_t, g - 1)
                link(add_halves(gate, MISC[:, 0:8 * E]))
                link(nc.vector.tensor_tensor(gate[:, :, :], gate[:, :, :], bg.unsqueeze(1).to_broadcast([P, 4, E]), ALU.add))
                link(nc.vector.tensor_tensor(ahead[:, :, :, :], gate[:, :, :].unsqueeze(2).to_broadcast([P, 4, E, E]),
                                             gate[:, :, :].unsqueeze(3).to_broadcast([P, 4, E, E]), ALU.subtract))
                flat = ahead[:, :, :, :].rearrange("p i e j -> p i (e j)")
                link(nc.vector.scalar_tensor_tensor(tied[:, :, :], flat, 0.0, before.unsqueeze(1).to_broadcast([P, 4, E * E]),
                                                    op0=ALU.is_equal, op1=ALU.mult))
                link(nc.vector.scalar_tensor_tensor(beaten[:, :, :], flat, 0.0, tied[:, :, :], op0=ALU.is_gt, op1=ALU.add))
                link(nc.vector.tensor_reduce(rank[:, :, :], beaten[:, :, :].rearrange("p i (e j) -> p i e j", e=E),
                                             axis=AX_X, op=ALU.add))
                for low in (0, R_LOW):
                    nc.vector.tensor_scalar(hm[:, s, :, R_SEL + low:R_SEL + low + E], rank[:, :, :], 1.5, None, ALU.is_lt)
                nc.vector.tensor_scalar(hm[:, s, :, R_OFF:R_OFF + E], rank[:, :, :], 1.5, None, ALU.is_gt).then_inc(mask_ready, 1)

            def norm2(g):
                if g >= 1:
                    dve.wait_ge(fin_ready, g)
                if g < G - 1:
                    dve.wait_ge(y_done, g + 1)
                    add_halves(res2, PV).then_inc(y_read, 1)
                    dve.wait_ge(y_read, g + 1)
                    sums = (res2[:, 0:2, :], res2[:, 2:4, :])
                    statistics(bst2, mv2, res2)
                else:
                    sums = [dst[:, 0:2 * D].rearrange("p (i d) -> p i d", d=D) for _, dst in y_parts(g)]
                    for i in range(4):
                        if i % 2 == 0:
                            dve.wait_ge(y_done, g + 1 + i // 2)
                        last = nc.vector.bn_stats(bst2[:, i, :], sums[i // 2][:, i % 2, :])
                    link(last)
                    aggregate(mv2, bst2)
                centre_and_root(res2, sums, nw2, mv2)
                nc.vector.tensor_tensor(fin[:, g, :, :], res2[:, :, :],
                                        nw2[:, :, 1].unsqueeze(2).to_broadcast([P, 4, D]), ALU.mult).then_inc(fin_ready, 1)

            def group_work(step, place):
                for at, where, what, g in ON_VECTOR:
                    if (at, where) == (step, place):
                        {"ctx": residual1, "stats": statistics1, "norm": norm1, "split": split_h1,
                         "gates": choose, "out": norm2}[what](g)

            tok_weights(0)
            x_low(0, (0,))
            tok_weights(1)
            x_low(0, (2,))
            x_low(1)
            x_low(2, (0,))
            emb(0)
            x_low(3)
            emb(1)
            emb(2)
            emb(3)
            dve.wait_ge(scaled, 1)
            low_parts(0, 0)
            low_parts(0, 1)
            v_emb(0, 0)
            v_emb(0, 1)
            rowmax(0)
            rowmax(1)
            low_parts(1, 0)
            for step in range(STEPS):
                group_work(step, 0)
                if step + 2 < NT:
                    rowmax(step + 2)
                if step == 0:
                    low_parts(1, 1)
                if step in V_STEPS:
                    v_emb(1, V_STEPS.index(step))
                group_work(step, 1)
            norm2(G - 1)

        @block.gpsimd
        def _(pool):
            chain = [0]

            def link(ins):
                chain[0] += 1
                ins.then_inc(pchain, 1)
                pool.wait_ge(pchain, chain[0])

            nc.gpsimd.memset(idle[:, :], 0.0).then_inc(idle_ready, 1)
            nc.gpsimd.memset(padw_hi[:, 0:D].bitcast(F32), 0.0)
            nc.gpsimd.memset(padw_lo[:, 0:D].bitcast(F32), 0.0).then_inc(padw_zero, 1)
            link(nc.gpsimd.memset(hm[:, :, :, D:P], 0.0))
            hm_lo = hm[:, :, :, D:P].rearrange("p a i (z n) -> p a i z n", n=R_LOW)
            for a in range(2):
                nc.gpsimd.memset(hm_lo[:, a, :, :, R_ONE - D], 1.0).then_inc(consts, 1)
            pool.wait_ge(consts, 2)
            k, rr = POOL_X
            b, m = k // 2, 8 * (k % 2)
            part = (slice(0, P), b, slice(m, m + 8), slice(rr, rr + 2))
            pool.wait_ge(xhi_ready, 2 * k + rr // 2 + 1)
            nc.gpsimd.tensor_tensor(x_lo[part], x_sb[part], x_hi[part].bitcast(F32), ALU.subtract).then_inc(xlo_pool, 1)
            pool.wait_ge(ld_attn, 16)
            nc.gpsimd.tensor_scalar(bq_s[:, :], bq, D ** -0.5, None, ALU.mult).then_inc(scaled, 1)
            link(nc.gpsimd.tensor_scalar(wq_s[:, :], wq2, D ** -0.5, None, ALU.mult))
            raw = (wq_s[:, :], wk2, wv_i)
            for w in range(3):
                link(nc.gpsimd.tensor_copy(projw_hi[:, w, :], raw[w]))
                nc.gpsimd.tensor_tensor(projw_lo[:, w, :], raw[w], projw_hi[:, w, :].bitcast(F32), ALU.subtract)\
                    .then_inc(projw_ready, 1)
            link(nc.gpsimd.tensor_copy(wg_r[:, 0:E], wg2))
            nc.gpsimd.tensor_tensor(wg_r[:, E:2 * E], wg2, wg_r[:, 0:E].bitcast(F32), ALU.subtract).then_inc(wg_ready, 1)
            pool.wait_ge(ld_ffn, 16)
            link(nc.gpsimd.tensor_copy(b2_r[:, :], b2_raw))
            link(nc.gpsimd.tensor_copy(w1_lo[D:P, :, :], w1b_raw[D:P, :, :]))
            link(nc.gpsimd.tensor_copy(w1_hi[:, :, :], w1_raw))
            link(nc.gpsimd.tensor_tensor(b2_r[96:P, :], b2_raw[96:P, :], b2_r[96:P, :].bitcast(F32), ALU.subtract))
            link(nc.gpsimd.tensor_tensor(w1_lo[96:P, :, :], w1b_raw[96:P, :, :], w1_lo[96:P, :, :].bitcast(F32), ALU.subtract))
            nc.gpsimd.tensor_tensor(w1_lo[0:D, :, :], w1b_raw[0:D, :, :], w1_hi[0:D, :, :].bitcast(F32), ALU.subtract)\
                .then_inc(ffnw, 1)
            pool.wait_ge(ffnw, 1)

            def inverse_root(g):
                pool.wait_ge(mv_ready, g + 1)
                a, y, z = nw[:, :, 0], nw[:, :, 1], nw[:, :, 2]
                link(nc.gpsimd.tensor_scalar(a, mv[:, :, 1], EPS, None, ALU.add))
                link(nc.gpsimd.tensor_scalar(y.bitcast(I32), a.bitcast(I32), -0.5, RSQRT_MAGIC, ALU.mult, ALU.add))
                for c3, c1 in NEWTON:
                    link(nc.gpsimd.tensor_tensor(z, y, y, ALU.mult))
                    link(nc.gpsimd.tensor_tensor(z, z, a, ALU.mult))
                    link(nc.gpsimd.tensor_scalar(z, z, -c3, c1, ALU.mult, ALU.add))
                    ins = nc.gpsimd.tensor_tensor(y, z, y, ALU.mult)
                    if c1 == NEWTON[-1][1]:
                        ins.then_inc(root_ready, 1)
                    else:
                        link(ins)

            for g in range(G):
                if g < POOL_ROOTS:
                    inverse_root(g)
                pool.wait_ge(h1_ready, g + 1)
                if g >= 2:
                    pool.wait_ge(hm_t, g - 1)
                nc.gpsimd.tensor_copy(hm[:, g % 2, :, 0:D].bitcast(F32R), h1[:, 4 * g:4 * g + 4, :]).then_inc(h_high, 1)


def dft_columns():
    k, p = np.arange(NFREQ)[:, None], np.arange(PATCH)[None, :]
    angle = 2 * np.pi * k * p / PATCH
    coef = np.concatenate([np.cos(angle), -np.sin(angle)], 0) / np.sqrt(PATCH)
    cols = np.zeros((OI, NCOEF, 2, OI, 9))
    for i in range(OI):
        for q in range(2):
            for h in range(2):
                cols[i, :, q, i, 4 * h:4 * h + 4] = coef[:, 8 * h + 4 * q:8 * h + 4 * q + 4]
        cols[i, :, 1, i, 8] = coef[:, 8:16].sum(1)
    return cols.reshape(OI * NCOEF, 2 * OI * 9).astype(np.float32)


def kernel(**inputs):
    import concourse.bacc as bacc
    from concourse.bass_utils import run_bass_kernel_spmd

    a = {n.removeprefix("L0_"): np.ascontiguousarray(v) for n, v in inputs.items()}
    f4 = np.float32
    w = np.concatenate([a["tok_W"], np.zeros((OP - D, NCOEF * C), f4)], 0)
    w = w.reshape(O2, OI, NCOEF, C).transpose(1, 2, 0, 3).reshape(OI * NCOEF, O2 * C)
    tok_pack = np.concatenate([w, dft_columns()], 1)

    eye = np.eye(D, dtype=f4)
    before = np.tile(np.tril(np.ones((E, E), f4), -1).reshape(1, E * E), (P, 1))
    two = lambda m: np.concatenate([m, m], 0)
    rows = lambda m: np.tile(m.reshape(1, -1), (P, 1))
    attn_pack = np.zeros((P, PA_N), f4)
    attn_pack[:, PA_ID:PA_ID + P] = np.eye(P, dtype=f4)
    attn_pack[:, PA_II:PA_II + D] = two(eye)
    for at, m in ((PA_WQ, a["attn_Wq"]), (PA_WK, a["attn_Wk"])):
        attn_pack[:, at:at + P] = np.concatenate([two(m), two(m)], 1)
    attn_pack[:, PA_WV:PA_WV + P] = np.concatenate([two(a["attn_Wv"]), two(eye)], 1)
    attn_pack[:, PA_BV:PA_BV + D] = rows(a["attn_bv"])
    attn_pack[:, PA_BQ] = two(a["attn_bq"])
    attn_pack[:, PA_BK] = two(a["attn_bk"])
    attn_pack[:, PA_WG:PA_WG + E] = two(a["ffn_Wg"])
    attn_pack[:, PA_BG:PA_BG + E] = rows(a["ffn_bg"])
    attn_pack[:, PA_LT:PA_LT + E * E] = before

    ffn_pack = np.zeros((P, PB_N), f4)
    w1 = a["ffn_W1"].transpose(1, 0, 2).reshape(D, E * H)
    ffn_pack[:, PB_W1:PB_W1 + E * H] = two(w1)
    ffn_pack[0:D, PB_W1B:PB_W1B + E * H] = w1
    off = np.zeros((E, E, H), f4)
    off[np.arange(E), np.arange(E), :] = -BIG
    for low in (0, R_LOW):
        ffn_pack[R_OFF + low:R_OFF + low + E, PB_W1B:PB_W1B + E * H] = off.reshape(E, E * H)
        ffn_pack[R_ONE + low, PB_W1B:PB_W1B + E * H] = a["ffn_b1"].reshape(-1)
        ffn_pack[R_SEL + low:R_SEL + low + E, PB_B2:PB_B2 + D] = a["ffn_b2"]
    ffn_pack[:, PB_W2:PB_W2 + E * D] = a["ffn_W2"].transpose(1, 0, 2).reshape(H, E * D)

    nc = bacc.Bacc("TRN2", target_bir_lowering=False, num_devices=1)
    arrays = {"x_dram": a["x"], "tok_pack": tok_pack, "attn_pack": attn_pack, "ffn_pack": ffn_pack}
    args = [nc.dram_tensor(n, v.shape, F32, kind="ExternalInput").ap() for n, v in arrays.items()]
    args.append(nc.dram_tensor("out_dram", (B, S, D), F32, kind="ExternalOutput").ap())
    vit_layer(nc, *args)
    r = run_bass_kernel_spmd(nc, [arrays], core_ids=[0])
    return r.results[0]["out_dram"]
```
